# Optimizing a Trainium2 kernel written in Bass

```python
import numpy as np
import jax
import jax.numpy as jnp

def _softmax(x, axis=-1):
    return jax.nn.softmax(x, axis=axis)

def _gelu(x):
    return jax.nn.gelu(x, approximate=True)

def _silu(x):
    return jax.nn.silu(x)

def _sigmoid(x):
    return jax.nn.sigmoid(x)

def _layernorm(x, axis=-1, eps=1e-05):
    m = jnp.mean(x, axis=axis, keepdims=True)
    v = jnp.var(x, axis=axis, keepdims=True)
    return (x - m) / jnp.sqrt(v + eps)

def _scatter_add(tgt, idx, src, axis=0):
    return tgt.at[idx].add(src)

def _segment_sum(src, seg, n):
    return jax.ops.segment_sum(src, seg, n)
kernel_name = 'mk_xattn_ffn_d2_seqx_r8_87a907'

def setup_inputs(seed: int=0):
    np.random.seed(seed)
    _w = jnp.asarray

    def _rec_inputs():
        import jax
        import jax.numpy as jnp
        _rk = jax.random.key(seed)
        x = 7.22e-05 + 1 * jax.random.normal(jax.random.fold_in(_rk, 1), (16, 128, 128), jnp.float32)
        _lenS = 128 - jax.random.randint(jax.random.fold_in(_rk, 7), (16,), 0, max(1, 128 // 4) + 1, jnp.int32)
        _lenS2 = 128 - jax.random.randint(jax.random.fold_in(_rk, 8), (16,), 0, max(1, 128 // 4) + 1, jnp.int32)
        _ctx_1024P = jax.random.normal(jax.random.fold_in(_rk, 11), (16, 16, 128), jnp.float32)
        _ctx_1024c = jax.random.dirichlet(jax.random.fold_in(_rk, 511), 0.3 * jnp.ones((16,), jnp.float32), (16, 128))
        _ctx_1024t = jnp.einsum('bsk,bkd->bsd', _ctx_1024c, _ctx_1024P)
        _ctx_1024t = _ctx_1024t * jax.lax.rsqrt(jnp.mean(jnp.square(_ctx_1024t)) + 1e-12) * 0.953939
        ctx_1024 = 4.13588e-05 + 0.999923 * (_ctx_1024t + 0.3 * jax.random.normal(jax.random.fold_in(_rk, 611), (16, 128, 128), jnp.float32))
        return (x, ctx_1024)
    x, ctx_1024 = _rec_inputs()

    def _L0_xattn_setup():
        import jax, jax.numpy as jnp
        import numpy as np
        B, L, D, H = (4, 256, 128, 16)
        HD = D // H
        SCALE = 1.0 / (D / H) ** 0.5

        def _split_heads(x):
            b, l, _ = x.shape
            return x.reshape(b, l, H, HD).transpose(0, 2, 1, 3)
        key = jax.random.key(seed)
        ks = jax.random.split(key, 11)
        s = 1.0 / np.sqrt(D)
        return {'q': jax.random.normal(ks[0], (B, L, D), jnp.float32), 'k': jax.random.normal(ks[1], (B, L, D), jnp.float32), 'v': jax.random.normal(ks[2], (B, L, D), jnp.float32), 'Wq': jax.random.normal(ks[3], (D, D), jnp.float32) * s, 'bq': jnp.zeros((D,), jnp.float32), 'Wk': jax.random.normal(ks[4], (D, D), jnp.float32) * s, 'bk': jnp.zeros((D,), jnp.float32), 'Wv': jax.random.normal(ks[5], (D, D), jnp.float32) * s, 'bv': jnp.zeros((D,), jnp.float32), 'Wo': jax.random.normal(ks[6], (D, D), jnp.float32) * s, 'bo': jnp.zeros((D,), jnp.float32)}
    _L0_xattn_all = _L0_xattn_setup()
    _L0_xattn_in = {k: v for k, v in _L0_xattn_all.items() if k in ('Wq', 'bq', 'Wk', 'bk', 'Wv', 'bv', 'Wo', 'bo')}
    del _L0_xattn_all

    def _L0_ffn_setup():
        import jax, jax.numpy as jnp
        import numpy as np
        B, S, DIM = (4, 256, 128)
        E, K, HID = (8, 2, 512)
        key = jax.random.key(seed)
        ks = jax.random.split(key, 8)
        init = lambda k, sh: jax.random.normal(k, sh, jnp.float32) * 0.02
        return {'x': jax.random.normal(ks[0], (B, S, DIM), jnp.float32), 'gate_w': init(ks[1], (DIM, E)), 'gate_b': jnp.zeros((E,), jnp.float32), 'w1': init(ks[2], (E, DIM, HID)), 'b1': jnp.zeros((E, HID), jnp.float32), 'w2': init(ks[3], (E, HID, DIM)), 'b2': jnp.zeros((E, DIM), jnp.float32), 'ws1': init(ks[4], (DIM, HID)), 'bs1': jnp.zeros((HID,), jnp.float32), 'ws2': init(ks[5], (HID, DIM)), 'bs2': jnp.zeros((DIM,), jnp.float32)}
    _L0_ffn_all = _L0_ffn_setup()
    _L0_ffn_in = {k: v for k, v in _L0_ffn_all.items() if k in ('gate_w', 'gate_b', 'w1', 'b1', 'w2', 'b2', 'ws1', 'bs1', 'ws2', 'bs2')}
    del _L0_ffn_all

    def _L1_xattn_setup():
        import jax, jax.numpy as jnp
        import numpy as np
        HEADS = 16
        DIM_HEAD = 64
        QUERY_DIM = 128
        CTX_DIM = 128
        INNER = HEADS * DIM_HEAD
        key = jax.random.key(seed)
        ks = jax.random.split(key, 7)
        B, N, M = (2, 256, 256)
        s = 0.02
        return {'x': jax.random.normal(ks[0], (B, N, QUERY_DIM), dtype=jnp.float32), 'context': jax.random.normal(ks[1], (B, M, CTX_DIM), dtype=jnp.float32), 'Wq': jax.random.normal(ks[2], (QUERY_DIM, INNER), dtype=jnp.float32) * s, 'Wk': jax.random.normal(ks[3], (CTX_DIM, INNER), dtype=jnp.float32) * s, 'Wv': jax.random.normal(ks[4], (CTX_DIM, INNER), dtype=jnp.float32) * s, 'Wo': jax.random.normal(ks[5], (INNER, QUERY_DIM), dtype=jnp.float32) * s, 'bo': jnp.zeros((QUERY_DIM,), dtype=jnp.float32)}
    _L1_xattn_all = _L1_xattn_setup()
    _L1_xattn_in = {k: v for k, v in _L1_xattn_all.items() if k in ('Wq', 'Wk', 'Wv', 'Wo', 'bo')}
    del _L1_xattn_all

    def _L1_ffn_setup():
        import jax, jax.numpy as jnp
        import numpy as np
        TOP_K = 2
        key = jax.random.key(seed)
        ks = jax.random.split(key, 5)
        B, S, D, H, E = (2, 256, 128, 352, 8)
        x = jax.random.normal(ks[0], (B, S, D), dtype=jnp.float32)
        Wg = jax.random.normal(ks[1], (E, D), dtype=jnp.float32) * 0.02
        W1 = jax.random.normal(ks[2], (E, H, D), dtype=jnp.float32) * 0.02
        W2 = jax.random.normal(ks[3], (E, H, D), dtype=jnp.float32) * 0.02
        W3 = jax.random.normal(ks[4], (E, D, H), dtype=jnp.float32) * 0.02
        return {'x': x, 'Wg': Wg, 'W1': W1, 'W2': W2, 'W3': W3}
    _L1_ffn_all = _L1_ffn_setup()
    _L1_ffn_in = {k: v for k, v in _L1_ffn_all.items() if k in ('Wg', 'W1', 'W2', 'W3')}
    del _L1_ffn_all
    return {'x': x, 'ctx_1024': ctx_1024, 'L0_xattn_Wq': _L0_xattn_in['Wq'], 'L0_xattn_bq': _L0_xattn_in['bq'], 'L0_xattn_Wk': _L0_xattn_in['Wk'], 'L0_xattn_bk': _L0_xattn_in['bk'], 'L0_xattn_Wv': _L0_xattn_in['Wv'], 'L0_xattn_bv': _L0_xattn_in['bv'], 'L0_xattn_Wo': _L0_xattn_in['Wo'], 'L0_xattn_bo': _L0_xattn_in['bo'], 'L0_ffn_gate_w': _L0_ffn_in['gate_w'], 'L0_ffn_gate_b': _L0_ffn_in['gate_b'], 'L0_ffn_w1': _L0_ffn_in['w1'], 'L0_ffn_b1': _L0_ffn_in['b1'], 'L0_ffn_w2': _L0_ffn_in['w2'], 'L0_ffn_b2': _L0_ffn_in['b2'], 'L0_ffn_ws1': _L0_ffn_in['ws1'], 'L0_ffn_bs1': _L0_ffn_in['bs1'], 'L0_ffn_ws2': _L0_ffn_in['ws2'], 'L0_ffn_bs2': _L0_ffn_in['bs2'], 'L1_xattn_Wq': _L1_xattn_in['Wq'], 'L1_xattn_Wk': _L1_xattn_in['Wk'], 'L1_xattn_Wv': _L1_xattn_in['Wv'], 'L1_xattn_Wo': _L1_xattn_in['Wo'], 'L1_xattn_bo': _L1_xattn_in['bo'], 'L1_ffn_Wg': _L1_ffn_in['Wg'], 'L1_ffn_W1': _L1_ffn_in['W1'], 'L1_ffn_W2': _L1_ffn_in['W2'], 'L1_ffn_W3': _L1_ffn_in['W3']}

def reference(x, ctx_1024, L0_xattn_Wq, L0_xattn_bq, L0_xattn_Wk, L0_xattn_bk, L0_xattn_Wv, L0_xattn_bv, L0_xattn_Wo, L0_xattn_bo, L0_ffn_gate_w, L0_ffn_gate_b, L0_ffn_w1, L0_ffn_b1, L0_ffn_w2, L0_ffn_b2, L0_ffn_ws1, L0_ffn_bs1, L0_ffn_ws2, L0_ffn_bs2, L1_xattn_Wq, L1_xattn_Wk, L1_xattn_Wv, L1_xattn_Wo, L1_xattn_bo, L1_ffn_Wg, L1_ffn_W1, L1_ffn_W2, L1_ffn_W3):
    import jax
    import jax.numpy as jnp

    def _L0_xattn_ref(q, k, v, Wq, bq, Wk, bk, Wv, bv, Wo, bo):
        import jax, jax.numpy as jnp
        import numpy as np
        B, L, D, H = (4, 256, 128, 16)
        HD = D // H
        SCALE = 1.0 / (D / H) ** 0.5

        def _split_heads(x):
            b, l, _ = x.shape
            return x.reshape(b, l, H, HD).transpose(0, 2, 1, 3)
        qh = _split_heads(q @ Wq.T + bq)
        kh = _split_heads(k @ Wk.T + bk)
        vh = _split_heads(v @ Wv.T + bv)
        scores = jnp.einsum('bhqd,bhkd->bhqk', qh, kh) * SCALE
        attn = jax.nn.softmax(scores, axis=-1)
        out = jnp.einsum('bhqk,bhkd->bhqd', attn, vh)
        out = out.transpose(0, 2, 1, 3).reshape(q.shape[0], q.shape[1], D)
        return out @ Wo.T + bo

    def _L0_ffn_ref(x, gate_w, gate_b, w1, b1, w2, b2, ws1, bs1, ws2, bs2):
        import jax, jax.numpy as jnp
        import numpy as np
        B, S, DIM = (4, 256, 128)
        E, K, HID = (8, 2, 512)
        orig_shape = x.shape
        xf = x.reshape(-1, DIM)
        logits = xf @ gate_w + gate_b
        top_w, top_i = jax.lax.top_k(logits, K)
        gw = jax.nn.softmax(top_w, axis=-1).astype(xf.dtype)
        combine = (gw[:, :, None] * jax.nn.one_hot(top_i, E, dtype=xf.dtype)).sum(axis=1)
        out = jnp.zeros_like(xf)
        for e in range(E):
            h = jax.nn.gelu(xf @ w1[e] + b1[e], approximate=False)
            out = out + combine[:, e:e + 1] * (h @ w2[e] + b2[e])
        shared = jax.nn.gelu(xf @ ws1 + bs1, approximate=False) @ ws2 + bs2
        return (out + shared).reshape(orig_shape)

    def _L1_xattn_ref(x, context, Wq, Wk, Wv, Wo, bo):
        import jax, jax.numpy as jnp
        import numpy as np
        HEADS = 16
        DIM_HEAD = 64
        QUERY_DIM = 128
        CTX_DIM = 128
        INNER = HEADS * DIM_HEAD
        B, N, _ = x.shape
        M = context.shape[1]
        scale = DIM_HEAD ** (-0.5)
        q = (x @ Wq).reshape(B, N, HEADS, DIM_HEAD).transpose(0, 2, 1, 3)
        k = (context @ Wk).reshape(B, M, HEADS, DIM_HEAD).transpose(0, 2, 1, 3)
        v = (context @ Wv).reshape(B, M, HEADS, DIM_HEAD).transpose(0, 2, 1, 3)
        sim = jnp.einsum('bhid,bhjd->bhij', q, k) * scale
        attn = jax.nn.softmax(sim, axis=-1)
        out = jnp.einsum('bhij,bhjd->bhid', attn, v)
        out = out.transpose(0, 2, 1, 3).reshape(B, N, INNER)
        return out @ Wo + bo

    def _L1_ffn_ref(x, Wg, W1, W2, W3):
        import jax, jax.numpy as jnp
        import numpy as np
        TOP_K = 2
        B, S, D = x.shape
        E = Wg.shape[0]
        xt = x.reshape(B * S, D)
        scores = xt @ Wg.T
        topk_scores, topk_idx = jax.lax.top_k(scores, TOP_K)
        gate = jax.nn.silu(jnp.einsum('td,ehd->teh', xt, W1))
        up = jnp.einsum('td,ehd->teh', xt, W2)
        y = jnp.einsum('teh,edh->ted', gate * up, W3)
        onehot = jax.nn.one_hot(topk_idx, E, dtype=x.dtype)
        w = jnp.einsum('tke,tk->te', onehot, topk_scores)
        out = jnp.einsum('te,ted->td', w, y)
        return out.reshape(B, S, D)
    x = x + _L0_xattn_ref(_layernorm(x, axis=-1), ctx_1024, ctx_1024, L0_xattn_Wq, L0_xattn_bq, L0_xattn_Wk, L0_xattn_bk, L0_xattn_Wv, L0_xattn_bv, L0_xattn_Wo, L0_xattn_bo)
    x = x + _L0_ffn_ref(_layernorm(x, axis=-1), L0_ffn_gate_w, L0_ffn_gate_b, L0_ffn_w1, L0_ffn_b1, L0_ffn_w2, L0_ffn_b2, L0_ffn_ws1, L0_ffn_bs1, L0_ffn_ws2, L0_ffn_bs2)
    x = x + _L1_xattn_ref(_layernorm(x, axis=-1), ctx_1024, L1_xattn_Wq, L1_xattn_Wk, L1_xattn_Wv, L1_xattn_Wo, L1_xattn_bo)
    x = x + _L1_ffn_ref(_layernorm(x, axis=-1), L1_ffn_Wg, L1_ffn_W1, L1_ffn_W2, L1_ffn_W3)
    return x

_drawn_inputs = setup_inputs


def setup_inputs(seed=0):
    import zlib

    import numpy as np

    out = dict(_drawn_inputs(seed))
    spreads = {'L0_xattn_bq': (0.0, 0.344),
     'L0_xattn_bk': (0.0, 0.8),
     'L0_xattn_bv': (0.0, 0.1),
     'L0_xattn_bo': (0.0, 0.1),
     'L0_ffn_gate_b': (0.0, 0.1),
     'L0_ffn_b1': (0.0, 0.564),
     'L0_ffn_b2': (0.0, 0.1),
     'L0_ffn_bs1': (0.0, 0.43),
     'L0_ffn_bs2': (0.0, 0.1),
     'L1_xattn_bo': (0.0, 0.1)}
    factors = {'L1_xattn_Wq': 8.0,
     'L1_xattn_Wk': 8.0,
     'L1_ffn_Wg': 8.0,
     'L1_ffn_W1': 8.0,
     'L1_ffn_W2': 8.0,
     'L1_ffn_W3': 8.0}
    for name, (base, spread) in spreads.items():
        noise = np.random.default_rng([zlib.crc32(name.encode()), seed]).standard_normal(out[name].shape)
        drawn = base * np.exp(spread * noise) if base else spread * noise
        out[name] = jnp.asarray(drawn.astype(out[name].dtype))
    for name, factor in factors.items():
        out[name] = (out[name] * factor).astype(out[name].dtype)
    return out
```

```python
from contextlib import ExitStack

import numpy as np

import concourse.bass as bass
from concourse import mybir

F32 = mybir.dt.float32
F32R = mybir.dt.float32r
U32 = mybir.dt.uint32
ALU = mybir.AluOpType
ACT = mybir.ActivationFunctionType
AX_X = mybir.AxisListType.X

B, S, D = 16, 128, 128
TOK = B * S
H = 16
HD0, HD1 = 8, 64
INNER1 = H * HD1
E = 8
HID0, HID1 = 512, 352
E0 = E + 1
EPS = 1e-5

GROUP = 512
NGROUP = TOK // GROUP
BPG = GROUP // S
QUADS = H // 4
UNITS = QUADS * BPG
SCALE0 = 1.0 / (D / H) ** 0.5
SCALE1 = HD1 ** -0.5
JOBS0 = HID0 // 128
JOBS1 = -(-HID1 // 128)
RING = 4



def span(start, size):
    return slice(start, start + size) if isinstance(start, int) else bass.ds(start, size)


def until(eng, sem, value):
    if not isinstance(value, int) or value > 0:
        eng.wait_ge(sem, value)


def side_jobs(layer):
    at = {-1: [], NGROUP * UNITS: []}
    for n in range(NGROUP * UNITS):
        g, u = divmod(n, UNITS)
        at[n] = []
        if layer == 0:
            if u == 0 and g:
                at[n].append(("V", BPG * g + 3))
            if u >= 13 and g < NGROUP - 1:
                at[n].append(("V", BPG * (g + 1) + u - 13))
        elif 1 <= n < NGROUP * UNITS - 3:
            at[n].append(("V", n + 3))
        if g and 1 <= u <= BPG:
            at[n].append(("O", BPG * (g - 1) + u - 1))
    at[-1] = [("V", b) for b in range(BPG)]
    at[NGROUP * UNITS] = [("O", BPG * (NGROUP - 1) + b) for b in range(BPG)]
    return at


def build(nc, a, out):
    c_dram = nc.dram_tensor("gates_by_expert", [2, E, TOK], F32, kind="Internal").ap()

    with ExitStack() as ctx:
        def sb(name, shape, dt=F32, stack=ctx):
            return stack.enter_context(nc.sbuf_tensor(name, shape, dt))

        def sem(name):
            return ctx.enter_context(nc.semaphore(name))

        bank = [ctx.enter_context(nc.psum_tensor(f"bank{i}", [128, GROUP], F32)) for i in range(8)]

        x = sb("x", [128, TOK])
        xn = sb("xn", [128, TOK])
        xt = sb("xt", [128, TOK])
        xt_hi = sb("xt_hi", [128, TOK], F32R)
        xt_lo = sb("xt_lo", [128, TOK], F32R)
        ct = sb("ct", [128, TOK])
        ct_hi = sb("ct_hi", [128, TOK], F32R)
        ct_lo = sb("ct_lo", [128, TOK], F32R)
        y = sb("y", [128, TOK])
        ident = sb("ident", [128, 128])
        expert_no = sb("expert_no", [128, E * B])
        masks = sb("masks", [128, 6])
        stats = sb("stats", [128, B * 6])
        meanvar = sb("meanvar", [128, B * 2])
        veps = sb("veps", [128, B])
        minus_half = sb("minus_half", [128, B])
        rstd = sb("rstd", [128, B])
        gw = [sb(f"gw{l}", [128, E]) for l in range(2)]
        gb = sb("gb", [128, E])
        logit = sb("logit", [128, B * E])
        top = sb("top", [128, B * 8])
        topi = sb("topi", [128, B * 8], U32)
        topf = sb("topf", [128, B * 2])
        gdiff = sb("gdiff", [128, B])
        gexp = sb("gexp", [128, B])
        gone = sb("gone", [128, B])
        gweight = sb("gweight", [128, 2 * B])
        hot1 = sb("hot1", [128, E * B])
        hot2 = sb("hot2", [128, E * B])
        combine = sb("combine", [128, E * B])
        combine_t = sb("combine_t", [128, 128])
        zeros = sb("zeros", [128, HID0])
        b2 = sb("b2", [128, E0])
        bo = [sb(f"bo{l}", [128, D]) for l in range(2)]
        negmax = sb("negmax", [128, 4 * 4])
        total = sb("total", [128, 4 * 4])
        rtotal = sb("rtotal", [128, 4 * 4])

        loaded = sem("loaded")
        ctx_split = sem("ctx_split")
        dve = sem("dve")
        pow_done = sem("pow_done")
        norm_in = sem("norm_in")
        xn_ready = sem("xn_ready")
        xt_ps = sem("xt_ps")
        xt_copied = sem("xt_copied")
        xt_ready = sem("xt_ready")
        bias_added = sem("bias_added")
        phase = sem("phase")
        table_ready = sem("table_ready")

        dve_n = [0]

        def seq(ins):
            dve_n[0] += 1
            ins.then_inc(dve, 1)
            return dve_n[0]

        def norm_vector(v, n):
            for t in range(B):
                k = seq(v.bn_stats(stats[:, t * 6:t * 6 + 6], x[:, t * D:(t + 1) * D]))
            v.wait_ge(dve, k)
            for t in range(B):
                k = seq(v.bn_aggr(meanvar[:, 2 * t:2 * t + 2], stats[:, t * 6:t * 6 + 6]))
            v.wait_ge(dve, k)
            var = meanvar[:, :].rearrange("p (t k) -> p t k", k=2)[:, :, 1]
            v.tensor_scalar(veps[:, :], var, EPS, None, ALU.add).then_inc(norm_in, 1)
            v.wait_ge(pow_done, n + 1)
            for t in range(B):
                v.tensor_scalar(xn[:, t * D:(t + 1) * D], x[:, t * D:(t + 1) * D],
                                meanvar[:, 2 * t:2 * t + 1], rstd[:, t:t + 1],
                                ALU.subtract, ALU.mult).then_inc(xn_ready, 1)
            for g in range(NGROUP):
                cols = slice(g * GROUP, (g + 1) * GROUP)
                v.wait_ge(xt_copied, NGROUP * n + g + 1)
                k = seq(v.tensor_copy(xt_hi[:, cols], xt[:, cols]))
                v.wait_ge(dve, k)
                v.tensor_tensor(xt_lo[:, cols], xt[:, cols], xt_hi[:, cols].bitcast(F32),
                                ALU.subtract).then_inc(xt_ready, 1)

        def norm_pool(p, n):
            p.wait_ge(norm_in, n + 1)
            p.tensor_tensor(rstd[:, :], veps[:, :], minus_half[:, :], ALU.pow).then_inc(pow_done, 1)

        def norm_tensor(pe, n):
            for g in range(NGROUP):
                if g >= 2:
                    pe.wait_ge(xt_copied, NGROUP * n + g - 1)
                for b in range(BPG):
                    t = g * BPG + b
                    pe.wait_ge(xn_ready, B * n + t + 1)
                    ins = pe.transpose(bank[g % 2][:, b * 128:(b + 1) * 128], xn[:, t * D:(t + 1) * D], ident[:, :])
                ins.then_inc(xt_ps, 1)

        def norm_scalar(act, n):
            for g in range(NGROUP):
                act.wait_ge(xt_ps, NGROUP * n + g + 1)
                act.activation(xt[:, g * GROUP:(g + 1) * GROUP], bank[g % 2][:, :], ACT.Copy).then_inc(xt_copied, 1)

        class Attention:

            def __init__(self, l, stack):
                self.l = l
                n = f"{l}"
                s = lambda name: sem(name + n)
                self.w_loaded, self.w_split = s("w_loaded"), s("w_split")
                self.qk_ps, self.qk_copied, self.qk_ready = s("qk_ps"), s("qk_copied"), s("qk_ready")
                self.side_ps, self.side_done = s("side_ps"), s("side_done")
                self.scored, self.maxed, self.exped = s("scored"), s("maxed"), s("exped")
                self.inverted, self.normed = s("inverted"), s("normed")
                self.turned, self.turned_a, self.turned_v = s("turned"), s("turned_a"), s("turned_v")
                self.weighed, self.out_copied = s("weighed"), s("out_copied")
                self.cleared, self.k_copied = s("cleared"), s("k_copied")
                self.cols = QUADS * 128 if l == 0 else INNER1
                b_ = lambda name, shape, dt=F32: sb(name + n, shape, dt, stack)
                self.names = ("q", "k") if l == 0 else ("q", "k", "v")
                self.raw = {w: b_("raw_" + w, [128, self.cols]) for w in self.names}
                self.hi = {w: b_("hi_" + w, [128, self.cols], F32R) for w in self.names}
                self.lo = {w: b_("lo_" + w, [128, self.cols], F32R) for w in self.names}
                self.p = [b_(f"p{i}_", [128, 512]) for i in range(4)]
                self.pt = [b_(f"pt{i}_", [128, 512]) for i in range(2)]
                if l == 0:
                    self.wv, self.wo = b_("wv", [128, D]), b_("wo", [128, QUADS * D])
                    self.bq, self.bk, self.bv = b_("bq", [128, QUADS]), b_("bk", [128, QUADS]), b_("bv", [128, D])
                    self.bqs = b_("bqs", [128, QUADS])
                    self.q = [b_(f"q{i}_", [128, GROUP], F32R) for i in range(2)]
                    self.k = [b_(f"k{i}_", [128, BPG * 4 * S], F32R) for i in range(2)]
                    self.full = {w: b_("full" + w, [128, GROUP]) for w in "qk"}
                    self.half = b_("half", [128, GROUP], F32R)
                    self.kst = b_("kst", [128, GROUP], F32R)
                    self.v = b_("v", [128, BPG * H * 32])
                    self.ot = b_("ot", [128, QUADS * GROUP])
                else:
                    self.wo = b_("wo", [128, 8 * D])
                    self.q = [b_(f"q{i}_", [128, 2 * GROUP]) for i in range(2)]
                    self.k = [b_(f"k{i}_", [128, 2 * BPG * 2 * S]) for i in range(2)]
                    self.v = [b_(f"v{i}_", [128, BPG * 256]) for i in range(2)]
                    self.ot = b_("ot", [128, 8 * GROUP])
                self.qk_jobs = 2 if l == 0 else 4
                self.side_at = side_jobs(l)
                self.side_place = {}
                for n_ in sorted(self.side_at):
                    for job in self.side_at[n_]:
                        self.side_place[job] = len(self.side_place)
                self.out_per = 4 if l == 0 else 2

            def qk_at(self, n):
                r, k = n % 4, n // 4
                if self.l == 0:
                    at = {1: [(k + 2, 0)], 3: [(k + 2, 1)]}.get(r, [])
                else:
                    at = [(k + 2, r - 1)] if r else ([(k + 1, 3)] if k else [])
                return [(b, j) for b, j in at if b < QUADS * NGROUP]

        NU = NGROUP * UNITS

        def three(pe, ps, w_hi, w_lo, m_hi, m_lo):
            pe.matmul(ps, w_lo, m_hi, start=True, stop=False)
            pe.matmul(ps, w_hi, m_lo, start=False, stop=False)
            return pe.matmul(ps, w_hi, m_hi, start=False, stop=True)

        def att_tensor(pe, A):
            l = A.l
            qk_bank, side_bank = bank[6], bank[7]

            def qk_job(block, job):
                g, quad = divmod(block, QUADS)
                until(pe, A.qk_copied, A.qk_jobs * block + job)
                if l == 0:
                    w, at = "qk"[job], quad * 128
                else:
                    w, at = "qk"[job // 2], (2 * quad + job % 2) * 128
                hi, lo = (xt_hi, xt_lo) if w == "q" else (ct_hi, ct_lo)
                m = slice(g * GROUP, (g + 1) * GROUP)
                three(pe, qk_bank[:, :], A.hi[w][:, at:at + 128], A.lo[w][:, at:at + 128],
                      hi[:, m], lo[:, m]).then_inc(A.qk_ps, 1)

            def side_job(name, item):
                until(pe, A.side_done, A.side_place[name, item])
                if name == "V" and l == 0:
                    t = item
                    ins = pe.matmul(side_bank[:, 0:D], ct[:, t * S:(t + 1) * S], A.wv[:, :], start=True, stop=True)
                elif name == "V":
                    g, u = divmod(item, UNITS)
                    quad, b = divmod(u, BPG)
                    t = g * BPG + b
                    c, w = slice(t * S, (t + 1) * S), slice(quad * 256, (quad + 1) * 256)
                    ins = three(pe, side_bank[:, 0:256], ct_hi[:, c], ct_lo[:, c], A.hi["v"][:, w], A.lo["v"][:, w])
                else:
                    g, b = divmod(item, BPG)
                    pe.wait_ge(A.out_copied, (g + 1) * UNITS // A.out_per - (1 if l and b < 2 else 0))
                    parts = QUADS if l == 0 else 8
                    for i in range(parts):
                        ins = pe.matmul(side_bank[:, 0:D], A.ot[:, i * GROUP + b * S:i * GROUP + (b + 1) * S],
                                        A.wo[:, i * D:(i + 1) * D], start=(i == 0), stop=(i == parts - 1))
                ins.then_inc(A.side_ps, 1)

            def score(n):
                block, b = divmod(n, BPG)
                q, k = A.q[block % 2], A.k[block % 2]
                ps = bank[n % 2]
                if l == 0:
                    pe.wait_ge(A.qk_ready, 2 * (block + 1))
                else:
                    pe.wait_ge(A.qk_copied, 4 * (block + 1))
                until(pe, A.exped, n - 1)
                if l == 0:
                    ins = pe.matmul(ps[:, :], q[:, b * S:(b + 1) * S], k[:, b * 512:(b + 1) * 512],
                                    start=True, stop=True)
                else:
                    for pair in range(2):
                        at = (pair * BPG + b) * 256
                        ins = pe.matmul(ps[:, pair * 256:(pair + 1) * 256],
                                        q[:, pair * GROUP + b * S:pair * GROUP + (b + 1) * S],
                                        k[:, at:at + 256], start=True, stop=True)
                ins.then_inc(A.scored, 1)

            def turn(n):
                pe.wait_ge(A.normed, n + 1)
                until(pe, A.turned_v if n % 2 else A.turned_a, n // 2)
                for j in range(4):
                    ins = pe.transpose(bank[2 + n % 2][:, j * 128:(j + 1) * 128],
                                       A.p[n % 4][:, j * 128:(j + 1) * 128], ident[:, :])
                ins.then_inc(A.turned, 1)

            def weigh(n):
                block, b = divmod(n, BPG)
                quad = block % QUADS
                g = n // UNITS
                pe.wait_ge(A.turned_v if n % 2 else A.turned_a, n // 2 + 1)
                chunk = n // A.out_per
                ps = bank[4 + chunk % 2]
                if n % A.out_per == 0:
                    until(pe, A.out_copied, chunk - 1)
                v_item = BPG * g + b if l == 0 else n
                pe.wait_ge(A.side_done, A.side_place["V", v_item] + 1)
                pt = A.pt[n % 2]
                for j in range(4):
                    if l == 0:
                        at = (b * H + 4 * quad + j) * 32
                        ins = pe.matmul(ps[32 * j:32 * j + 32, b * 128:(b + 1) * 128], A.v[:, at:at + 32],
                                        pt[:, j * 128:(j + 1) * 128], start=True, stop=True)
                    else:
                        pair, half = divmod(j, 2)
                        at = b * 256 + j * 64
                        col = pair * 256 + (b % 2) * 128
                        ins = pe.matmul(ps[64 * half:64 * half + 64, col:col + 128],
                                        A.v[block % 2][:, at:at + 64],
                                        pt[:, j * 128:(j + 1) * 128], start=True, stop=True)
                ins.then_inc(A.weighed, 1)

            pe.wait_ge(A.w_split, len(A.names))
            pe.wait_ge(A.w_loaded, 16 * A.n_loads)
            for block in range(2):
                for job in range(A.qk_jobs):
                    qk_job(block, job)
                if block == 0:
                    for job in A.side_at[-1]:
                        side_job(*job)
            for n in range(3):
                score(n)
            for n in range(NU + 1):
                if n + 3 < NU:
                    score(n + 3)
                if n < NU:
                    turn(n)
                if n:
                    weigh(n - 1)
                if n < NU:
                    for job in A.qk_at(n):
                        qk_job(*job)
                for job in A.side_at[n]:
                    side_job(*job)

        def att_scalar(act, A):
            l = A.l

            def exps(n):
                act.wait_ge(A.maxed, n + 1)
                until(act, A.turned, n - 3)
                until(act, A.inverted, n - 3)
                for j in range(4):
                    col = (n % 4) * 4 + j
                    ins = act.activation(A.p[n % 4][:, j * 128:(j + 1) * 128],
                                         bank[n % 2][:, j * 128:(j + 1) * 128], ACT.Exp,
                                         bias=negmax[:, col:col + 1], scale=1.0, accum_out=total[:, col:col + 1])
                ins.then_inc(A.exped, 1)

            def copy_out(n):
                act.wait_ge(A.turned, n + 1)
                until(act, A.weighed, n - 1)
                act.activation(A.pt[n % 2][:, :], bank[2 + n % 2][:, :], ACT.Copy).then_inc(A.turned_a, 1)

            def qk_copy(block, job):
                quad = block % QUADS
                act.wait_ge(A.qk_ps, A.qk_jobs * block + job + 1)
                if l == 0:
                    w = "qk"[job]
                    until(act, A.qk_ready, 2 * block + job - 1)
                    act.activation(A.full[w][:, :], bank[6][:, :], ACT.Identity,
                                   bias=(A.bqs if w == "q" else A.bk)[:, quad:quad + 1],
                                   scale=SCALE0 if w == "q" else 1.0).then_inc(A.qk_copied, 1)
                    return
                until(act, A.scored, BPG * (block - 1))
                pair = job % 2
                if job < 2:
                    act.activation(A.q[block % 2][:, pair * GROUP:(pair + 1) * GROUP], bank[6][:, :], ACT.Copy,
                                   scale=SCALE1).then_inc(A.qk_copied, 1)
                    return
                k = A.k[block % 2][:, pair * 1024:(pair + 1) * 1024].rearrange("p (b h s) -> p b h s", b=BPG, h=2)
                ps = bank[6][:, :].rearrange("p (b s) -> p b s", b=BPG)
                if block < 2:
                    act.wait_ge(A.cleared, 1 + block)
                act.activation(k[0:64, :, 0, :], ps[0:64], ACT.Copy)
                act.activation(k[64:128, :, 1, :], ps[64:128], ACT.Copy).then_inc(A.qk_copied, 1)

            if l == 0:
                act.wait_ge(A.cleared, 2)
            for block in range(2):
                for job in range(A.qk_jobs):
                    qk_copy(block, job)
            for n in range(2):
                exps(n)
            for n in range(NU):
                if n + 2 < NU:
                    exps(n + 2)
                if n % 2 == 0:
                    copy_out(n)
                for job in A.qk_at(n):
                    qk_copy(*job)

        def att_pool(p, A):
            if A.l == 0:
                p.memset(A.v[:, :], 0.0).then_inc(A.cleared, 1)
            else:
                for i in range(2):
                    p.memset(A.k[i][:, :], 0.0).then_inc(A.cleared, 1)
            for w in A.names:
                p.wait_ge(A.w_loaded, 16 * A.n_loads)
                p.tensor_copy(A.hi[w][:, :], A.raw[w][:, :]).then_inc(pool_own, 1)
                pool_n[0] += 1
                p.wait_ge(pool_own, pool_n[0])
                p.tensor_tensor(A.lo[w][:, :], A.raw[w][:, :], A.hi[w][:, :].bitcast(F32),
                                ALU.subtract).then_inc(A.w_split, 1)
            for n in range(NU):
                s = (n % 4) * 4
                p.wait_ge(A.inverted, n + 1)
                pr = A.p[n % 4][:, :].rearrange("p (h s) -> p h s", h=4)
                p.tensor_tensor(pr, pr, rtotal[:, s:s + 4].rearrange("p (h o) -> p h o", o=1).to_broadcast([128, 4, 128]),
                                ALU.mult).then_inc(A.normed, 1)

        def att_vector(v, A):
            l = A.l

            def row_max(n):
                v.wait_ge(A.scored, n + 1)
                until(v, A.exped, n - 3)
                s = (n % 4) * 4
                v.tensor_reduce(negmax[:, s:s + 4], bank[n % 2][:, :].rearrange("p (h s) -> p h s", h=4),
                                AX_X, ALU.max, negate=True).then_inc(A.maxed, 1)

            def invert(n):
                v.wait_ge(A.exped, n + 1)
                until(v, A.normed, n - 3)
                s = (n % 4) * 4
                v.reciprocal(rtotal[:, s:s + 4], total[:, s:s + 4]).then_inc(A.inverted, 1)

            def copy_out(n):
                v.wait_ge(A.turned, n + 1)
                until(v, A.weighed, n - 1)
                v.tensor_copy(A.pt[n % 2][:, :], bank[2 + n % 2][:, :]).then_inc(A.turned_v, 1)

            def out_copy(chunk):
                v.wait_ge(A.weighed, A.out_per * (chunk + 1))
                g, c = divmod(chunk, UNITS // A.out_per)
                if g:
                    batches = BPG if l == 0 or c % 2 else 2
                    if c < (1 if l == 0 else 2):
                        v.wait_ge(A.side_ps, A.side_place["O", BPG * (g - 1) + batches - 1] + 1)
                ps = bank[4 + chunk % 2]
                if l == 0:
                    v.tensor_copy(A.ot[:, c * GROUP:(c + 1) * GROUP], ps[:, :]).then_inc(A.out_copied, 1)
                else:
                    quad, half = divmod(c, 2)
                    o = A.ot[:, 2 * quad * GROUP:(2 * quad + 2) * GROUP].rearrange("p (i s) -> p i s", i=2)
                    v.tensor_copy(o[:, :, half * 256:(half + 1) * 256],
                                  ps[:, :].rearrange("p (i s) -> p i s", i=2)).then_inc(A.out_copied, 1)

            def halves(block, job):
                w = "qk"[job]
                v.wait_ge(A.qk_copied, 2 * block + job + 1)
                until(v, A.scored, BPG * (block - 1))
                until(v, A.qk_ready, 2 * block + job)
                full = A.full[w]
                k = seq(v.tensor_scalar(A.half[:, :], full[:, :], masks[:, job:job + 1], None, ALU.mult))
                v.wait_ge(dve, k)
                if job == 0:
                    v.tensor_tensor(A.q[block % 2][:, :], full[:, :], A.half[:, :].bitcast(F32),
                                    ALU.subtract).then_inc(A.qk_ready, 1)
                    return
                k = seq(v.tensor_tensor(A.kst[:, :], full[:, :], A.half[:, :].bitcast(F32), ALU.subtract))
                v.wait_ge(dve, k)
                kk = A.k[block % 2][:, :].rearrange("p (b h s) -> p b h s", b=BPG, h=4)
                for j in range(4):
                    ins = (v.tensor_scalar(kk[:, :, j, :], A.kst[:, :].bitcast(F32).rearrange("p (b s) -> p b s", b=BPG),
                                            masks[:, 2 + j:3 + j], None, ALU.mult))
                ins.then_inc(A.qk_ready, 1)

            def side(name, item):
                v.wait_ge(A.side_ps, A.side_place[name, item] + 1)
                if name == "V" and l == 0:
                    b = item % BPG
                    until(v, A.weighed, UNITS * (item // BPG) - BPG + b + 1 if item >= BPG else 0)
                    if item < BPG:
                        v.wait_ge(A.cleared, 1)
                    vv = A.v[:, b * 512:(b + 1) * 512].rearrange("p (h c) -> p h c", h=H)[:, :, 0:HD0]
                    v.tensor_tensor(vv, bank[7][:, 0:D].rearrange("p (h c) -> p h c", h=H),
                                    A.bv[:, :].rearrange("p (h c) -> p h c", h=H), ALU.add).then_inc(A.side_done, 1)
                elif name == "V":
                    block, b = divmod(item, BPG)
                    until(v, A.weighed, item - 8 + 1)
                    v.tensor_copy(A.v[block % 2][:, b * 256:(b + 1) * 256], bank[7][:, 0:256]).then_inc(A.side_done, 1)
                else:
                    t = item
                    xs = x[:, t * D:(t + 1) * D]
                    v.tensor_tensor(xs, bank[7][:, 0:D], xs, ALU.add).then_inc(A.side_done, 1)

            if l == 0:
                v.wait_ge(A.w_loaded, 16 * A.n_loads)
                v.tensor_scalar(A.bqs[:, :], A.bq[:, :], SCALE0, None, ALU.mult).then_inc(A.cleared, 1)
                for block in range(2):
                    for job in range(2):
                        halves(block, job)
                    if block == 0:
                        for job in A.side_at[-1]:
                            side(*job)
            else:
                for job in A.side_at[-1]:
                    side(*job)
            for n in range(3):
                row_max(n)
            invert(0)
            for n in range(NU + 1):
                if n + 3 < NU:
                    row_max(n + 3)
                if n + 1 < NU:
                    invert(n + 1)
                if n < NU and n % 2:
                    copy_out(n)
                if n == NU:
                    out_copy(n // A.out_per - 1)
                if l == 0 and n < NU:
                    for job in A.qk_at(n):
                        halves(*job)
                for job in A.side_at[n]:
                    side(*job)
                if 0 < n < NU and n % A.out_per == 0:
                    out_copy(n // A.out_per - 1)
            v.wait_ge(A.side_done, len(A.side_place))
            v.sem_inc(phase, 1)

        router = {n: sem("router_" + n) for n in ("logits", "max", "exp", "ready", "turned", "copied", "stored")}

        def route_tensor(pe, l):
            pe.wait_ge(xt_copied, NGROUP * (2 * l + 2))
            for t in range(B):
                ins = pe.matmul(bank[6][:, t * E:(t + 1) * E], xt[:, t * S:(t + 1) * S], gw[l][:, :],
                                start=True, stop=True)
            ins.then_inc(router["logits"], 1)
            pe.wait_ge(router["ready"], l + 1)
            pe.transpose(bank[7][:, 0:128], combine[:, :], ident[:, :]).then_inc(router["turned"], 1)

        def route_vector(v, l):
            v.wait_ge(router["logits"], l + 1)
            lg = logit[:, :].rearrange("p (t e) -> p t e", e=E)
            ps = bank[6][:, 0:B * E].rearrange("p (t e) -> p t e", e=E)
            if l == 0:
                gbb = gb[:, :].rearrange("p (o e) -> p o e", o=1).to_broadcast([128, B, E])
                k = seq(v.tensor_tensor(lg, ps, gbb, ALU.add))
            else:
                k = seq(v.tensor_copy(lg, ps))
            v.wait_ge(dve, k)
            for t in range(B):
                k = seq(v.max(top[:, t * 8:(t + 1) * 8], logit[:, t * E:(t + 1) * E]))
            v.wait_ge(dve, k)
            for t in range(B):
                k = seq(v.max_index(topi[:, t * 8:(t + 1) * 8], top[:, t * 8:(t + 1) * 8],
                                    logit[:, t * E:(t + 1) * E]))
            v.wait_ge(dve, k)
            tops = top[:, :].rearrange("p (t k) -> p t k", k=8)
            two = lambda buf: buf[:, :].rearrange("p (t k) -> p t k", k=2)
            k = seq(v.tensor_copy(two(topf), topi[:, :].rearrange("p (t k) -> p t k", k=8)[:, :, 0:2]))
            w = two(gweight)
            if l == 0:
                k = seq(v.tensor_tensor(gdiff[:, :], tops[:, :, 1], tops[:, :, 0], ALU.subtract))
                v.wait_ge(dve, k)
                v.sem_inc(router["max"], 1)
                v.wait_ge(router["exp"], 1)
                k = seq(v.tensor_scalar(gone[:, :], gexp[:, :], 1.0, None, ALU.add))
                v.wait_ge(dve, k)
                k = seq(v.reciprocal(w[:, :, 0], gone[:, :]))
                v.wait_ge(dve, k)
                k = seq(v.tensor_tensor(w[:, :, 1], gexp[:, :], w[:, :, 0], ALU.mult))
            else:
                k = seq(v.tensor_copy(w, tops[:, :, 0:2]))
            v.wait_ge(dve, k)
            no = expert_no[:, :].rearrange("p (e t) -> p e t", t=B)
            col = lambda buf, i: two(buf)[:, :, i].rearrange("p (o t) -> p o t", o=1).to_broadcast([128, E, B])
            hots = [hot1[:, :].rearrange("p (e t) -> p e t", t=B), hot2[:, :].rearrange("p (e t) -> p e t", t=B)]
            for i in range(2):
                k = seq(v.tensor_tensor(hots[i], no, col(topf, i), ALU.is_equal))
            v.wait_ge(dve, k)
            for i in range(2):
                k = seq(v.tensor_tensor(hots[i], hots[i], col(gweight, i), ALU.mult))
            v.wait_ge(dve, k)
            v.tensor_tensor(combine[:, :], hot1[:, :], hot2[:, :], ALU.add).then_inc(router["ready"], 1)
            v.wait_ge(router["turned"], l + 1)
            v.tensor_copy(combine_t[:, :], bank[7][:, 0:128]).then_inc(router["copied"], 1)

        def route_scalar(act, l):
            if l == 0:
                act.wait_ge(router["max"], 1)
                act.activation(gexp[:, :], gdiff[:, :], ACT.Exp).then_inc(router["exp"], 1)

        def route_sync(sp, l):
            sp.wait_ge(router["copied"], l + 1)
            sp.dma_start(c_dram[l].rearrange("e (t s) -> (e t) s", t=B), combine_t[:, :]).then_inc(router["stored"], 16)
            sp.wait_ge(router["stored"], 16 * (l + 1))

        LAG = 3

        class Experts:
            def __init__(self, l, stack):
                self.l = l
                n = f"_x{l}"
                s = lambda name: sem(name + n)
                self.n = E0 if l == 0 else E
                self.nb = JOBS0 if l == 0 else JOBS1
                self.per = self.nb * NGROUP
                hid = HID0 if l == 0 else HID1
                self.width = lambda hb: min(128, hid - 128 * hb)
                self.parts = {"in": hid, "out": self.nb * 128}
                if l:
                    self.parts = {"in": hid, "up": hid, "out": self.nb * 128}
                b_ = lambda name, shape, dt=F32: sb(name + n, shape, dt, stack)
                self.raw = {w: b_("raw_" + w, [128, c]) for w, c in self.parts.items()}
                self.hi = [{w: b_(f"hi{i}_" + w, [128, c], F32R) for w, c in self.parts.items()} for i in range(2)]
                self.lo = [{w: b_(f"lo{i}_" + w, [128, c], F32R) for w, c in self.parts.items()} for i in range(2)]
                self.gate = [b_(f"gate{i}_", [128, TOK]) for i in range(2)]
                self.h = [b_(f"h{i}_", [128, GROUP]) for i in range(RING)]
                self.h_hi = [b_(f"hh{i}_", [128, GROUP], F32R) for i in range(RING)]
                self.h_lo = [b_(f"hl{i}_", [128, GROUP], F32R) for i in range(RING)]
                self.act = [b_(f"act{i}_", [128, GROUP]) for i in range(RING)] if l else None
                self.b1 = [b_(f"b1_{i}_", [128, JOBS0]) for i in range(2)]
                self.bias_in = [s("bias_in_a"), s("bias_in_b")]
                self.weighted = b_("weighted", [128, GROUP])
                self.w_in, self.split = s("w_in"), s("split")
                self.gate_in = [s("gate_in_a"), s("gate_in_b")]
                self.h_ps, self.acted, self.multiplied = s("h_ps"), s("acted"), s("multiplied")
                self.hi_done, self.lo_done, self.h_used = s("hi_done"), s("lo_done"), s("h_used")
                self.y_added, self.y_read, self.y_zero, self.raw_split = s("y_added"), s("y_read"), s("y_zero"), s("raw_split")

            def loop(self, eng, body):
                body(0, 2)
                with eng.Fori(1, self.n // 2) as p:
                    body(p, 2)
                if self.n % 2:
                    body(self.n // 2, 1)

        def ffn_sync(sp, X, srcs, l):
            def body(pair, n):
                e0 = 2 * pair
                for i in range(n):
                    e = e0 + i
                    until(sp, X.raw_split, len(X.parts) * e)
                    for w in X.parts:
                        sp.dma_start(X.raw[w][:, :], srcs[w][span(e * 128, 128), :]).then_inc(X.w_in, 16)
                    if l == 0:
                        until(sp, X.hi_done, X.per * (e - 1))
                        sp.dma_start(X.b1[i][:, :], srcs["bias"][span(e * 128, 128), :]).then_inc(X.bias_in[i], 16)
                    if isinstance(e, int) and e == E:
                        continue
                    until(sp, X.y_read, NGROUP * (e - 1))
                    row = c_dram[l, span(e, 1), :] if not isinstance(e, int) else c_dram[l, e:e + 1, :]
                    sp.dma_start(X.gate[i][:, :], row.to_broadcast([128, TOK])).then_inc(X.gate_in[i], 16)
            X.loop(sp, body)

        def ffn_pool(p, X):
            p.memset(y[:, :], 0.0).then_inc(X.y_zero, 1)
            p.wait_ge(pool_own, 1)

            def body(pair, n):
                e0 = 2 * pair
                for i in range(n):
                    e = e0 + i
                    p.wait_ge(X.w_in, 16 * len(X.parts) * (e + 1))
                    until(p, X.h_used, X.per * (e - 1))
                    for k, w in enumerate(X.parts):
                        p.tensor_tensor(X.hi[i][w][:, :], X.raw[w][:, :], zeros[:, 0:X.parts[w]],
                                        ALU.add).then_inc(X.split, 1)
                        p.wait_ge(X.split, len(X.parts) * e + k + 1)
                        p.tensor_tensor(X.lo[i][w][:, :], X.raw[w][:, :], X.hi[i][w][:, :].bitcast(F32),
                                        ALU.subtract).then_inc(X.raw_split, 1)
            X.loop(p, body)

        def ffn_tensor(pe, X):
            def hidden(e, i, j, base):
                tg, hb = divmod(j % X.per, X.nb)
                width = X.width(hb)
                m = slice(tg * GROUP, (tg + 1) * GROUP)
                c = slice(hb * 128, hb * 128 + width)
                if j % X.per == 0:
                    pe.wait_ge(X.raw_split, len(X.parts) * (e + 1))
                if X.l == 0:
                    until(pe, X.hi_done, base + j - 3)
                    three(pe, bank[j % 4][0:width, :], X.hi[i]["in"][:, c], X.lo[i]["in"][:, c],
                          xt_hi[:, m], xt_lo[:, m]).then_inc(X.h_ps, 1)
                else:
                    until(pe, X.multiplied, base + j - 1)
                    for k, w in enumerate(("in", "up")):
                        ins = three(pe, bank[2 * (j % 2) + k][0:width, :], X.hi[i][w][:, c], X.lo[i][w][:, c],
                                    xt_hi[:, m], xt_lo[:, m])
                    ins.then_inc(X.h_ps, 1)

            def outward(j, base, ubase):
                i = (j // X.per) % 2
                tg, hb = divmod(j % X.per, X.nb)
                width = X.width(hb)
                unit = j // X.nb
                ps = bank[4 + unit % 2]
                if hb == 0:
                    until(pe, X.y_read, ubase + unit - 1)
                pe.wait_ge(X.hi_done, base + j + 1)
                pe.wait_ge(X.lo_done, base + j + 1)
                wc = slice(hb * 128, (hb + 1) * 128)
                hi, lo = X.hi[i]["out"][0:width, wc], X.lo[i]["out"][0:width, wc]
                hh, hl = X.h_hi[j % RING][0:width, :], X.h_lo[j % RING][0:width, :]
                pe.matmul(ps[:, :], lo, hh, start=(hb == 0), stop=False)
                pe.matmul(ps[:, :], hi, hl, start=False, stop=False)
                pe.matmul(ps[:, :], hi, hh, start=False, stop=(hb == X.nb - 1)).then_inc(X.h_used, 1)

            def body(pair, n):
                e0 = 2 * pair
                base, ubase = X.per * e0, NGROUP * e0
                for j in range(n * X.per):
                    hidden(e0 + j // X.per, j // X.per, j, base)
                    if not (isinstance(e0, int) and e0 == 0 and j < LAG):
                        outward(j - LAG, base, ubase)
            X.loop(pe, body)
            total_jobs = X.per * X.n
            tail = X.n - 1 if X.n % 2 else X.n - 2
            for j in range(total_jobs - LAG, total_jobs):
                outward(j - X.per * tail, X.per * tail, NGROUP * tail)
            for t in range(B):
                if t % 4 == 0:
                    if t == 0:
                        pe.wait_ge(X.y_read, NGROUP * X.n)
                        pe.wait_ge(X.y_added, NGROUP * E)
                    elif t >= 8:
                        pe.wait_ge(x_added, NGROUP * X.l + t // 4 - 1)
                ins = pe.transpose(bank[6 + (t // 4) % 2][:, (t % 4) * 128:(t % 4 + 1) * 128],
                                   y[:, t * S:(t + 1) * S], ident[:, :])
                if t % 4 == 3:
                    ins.then_inc(y_turned, 1)

        def ffn_scalar(act, X):
            def body(pair, n):
                e0 = 2 * pair
                base = X.per * e0
                for j in range(n * X.per):
                    e, hb = e0 + j // X.per, j % X.nb
                    width = X.width(hb)
                    r = j % RING
                    act.wait_ge(X.h_ps, base + j + 1)
                    if X.l == 0:
                        bias = X.b1[j // X.per][:, hb:hb + 1]
                        if j % X.per == 0:
                            act.wait_ge(X.bias_in[j // X.per], pair * 16 + 16)
                        until(act, X.lo_done, base + j - 3)
                        act.activation(X.h[r][:, :], bank[r][:, :], ACT.Gelu, bias=bias).then_inc(X.acted, 1)
                        until(act, X.h_used, base + j - 3)
                        act.activation(X.h_hi[r][:, :], bank[r][:, :], ACT.Gelu, bias=bias).then_inc(X.hi_done, 1)
                        continue
                    until(act, X.multiplied, base + j - 3)
                    act.activation(X.act[r][0:width, :], bank[2 * (j % 2)][0:width, :], ACT.Silu).then_inc(X.acted, 1)
                    if not (isinstance(e0, int) and e0 == 0 and j == 0):
                        high(base, j - 1)
            def high(base, j):
                width, r = X.width(j % X.nb), j % RING
                act.wait_ge(X.multiplied, base + j + 1)
                until(act, X.h_used, base + j - 3)
                act.activation(X.h_hi[r][0:width, :], X.h[r][0:width, :], ACT.Copy).then_inc(X.hi_done, 1)
            X.loop(act, body)
            if X.l:
                high(0, X.per * X.n - 1)

        def ffn_vector(v, X):
            v.wait_ge(X.y_zero, 1)

            def low(base, j):
                width, r = X.width(j % X.nb), j % RING
                v.wait_ge(X.hi_done, base + j + 1)
                until(v, X.h_used, base + j - 3)
                v.tensor_tensor(X.h_lo[r][0:width, :], X.h[r][0:width, :], X.h_hi[r][0:width, :].bitcast(F32),
                                ALU.subtract).then_inc(X.lo_done, 1)

            def gather(p, j):
                e0, base, ubase = 2 * p, 2 * X.per * p, 2 * NGROUP * p
                unit = j // X.nb
                tg = unit % NGROUP
                i = (unit // NGROUP) % 2
                e = e0 + unit // NGROUP
                m = slice(tg * GROUP, (tg + 1) * GROUP)
                v.wait_ge(X.h_used, base + j + 1)
                ps = bank[4 + unit % 2]
                if isinstance(e, int) and e == E:
                    v.wait_ge(X.y_added, NGROUP * E)
                    v.scalar_tensor_tensor(out=y[:, m], in0=ps[:, :], scalar=b2[:, E:E + 1], in1=y[:, m],
                                           op0=ALU.add, op1=ALU.add).then_inc(X.y_read, 1)
                    return
                if tg == 0:
                    v.wait_ge(X.gate_in[i], 16 * p + 16)
                gate = X.gate[i][:, m]
                until(v, X.y_added, ubase + unit)
                if X.l == 0:
                    v.scalar_tensor_tensor(out=X.weighted[:, :], in0=ps[:, :], scalar=b2[:, span(e, 1)], in1=gate,
                                           op0=ALU.add, op1=ALU.mult).then_inc(X.y_read, 1)
                else:
                    v.tensor_tensor(X.weighted[:, :], ps[:, :], gate, ALU.mult).then_inc(X.y_read, 1)
                v.wait_ge(X.y_read, ubase + unit + 1)
                v.tensor_tensor(y[:, m], y[:, m], X.weighted[:, :], ALU.add).then_inc(X.y_added, 1)

            def body(p, n):
                base = 2 * X.per * p
                zero = isinstance(p, int) and p == 0
                for j in range(n * X.per):
                    if X.l == 0:
                        low(base, j)
                    else:
                        width, r = X.width(j % X.nb), j % RING
                        v.wait_ge(X.acted, base + j + 1)
                        until(v, X.hi_done, base + j - 3)
                        v.tensor_tensor(X.h[r][0:width, :], bank[2 * (j % 2) + 1][0:width, :], X.act[r][0:width, :],
                                        ALU.mult).then_inc(X.multiplied, 1)
                        if not (zero and j == 0):
                            low(base, j - 1)
                    done = j - LAG - 1
                    if (done + 1) % X.nb == 0 and not (zero and done < 0):
                        gather(p, done)
            X.loop(v, body)
            tail = X.n - 1 if X.n % 2 else X.n - 2
            rest = X.per * (X.n - tail)
            if X.l:
                low(X.per * tail, rest - 1)
            for done in range(rest - LAG - 1, rest):
                if (done + 1) % X.nb == 0:
                    gather(tail // 2, done)
            for g in range(NGROUP):
                v.wait_ge(y_turned, NGROUP * X.l + g + 1)
                m = slice(g * GROUP, (g + 1) * GROUP)
                v.tensor_tensor(x[:, m], bank[6 + g % 2][:, :], x[:, m], ALU.add).then_inc(x_added, 1)
            v.wait_ge(x_added, NGROUP * (X.l + 1))
            v.sem_inc(phase, 1)

        y_turned, x_added, finished = sem("y_turned"), sem("x_added"), sem("finished")
        pool_own = sem("pool_own")
        bo_ready = sem("bo_ready")
        pool_n = [1]
        stacks = [ctx.enter_context(ExitStack()) for _ in range(4)]
        parts = []
        for l in range(2):
            with ExitStack() as st:
                A = Attention(l, st)
            with ExitStack() as st:
                X = Experts(l, st)
            parts.append((A, X))

        def att_loads(l, A):
            if l == 0:
                return [(A.raw["q"][:, :], a["wq0"]), (A.raw["k"][:, :], a["wk0"]), (A.wv[:, :], a["wv0"]),
                        (A.wo[:, :], a["wo0"]), (A.bq[:, :], a["bq"]), (A.bk[:, :], a["bk"]),
                        (A.bv[:, :], a["bv"].to_broadcast([128, D]))]
            return [(A.raw["q"][:, :], a["wq1"]), (A.raw["k"][:, :], a["wk1"]), (A.raw["v"][:, :], a["wv1"]),
                    (A.wo[:, :], a["wo1"])]

        first_loads = [(masks, "masks"), (ident, "ident"), (minus_half, "minus_half"), (expert_no, "expert_no"),
                       (gw[0], "gw0"), (gw[1], "gw1"), (b2, "b2"), (ct, "ct")]
        for l in range(2):
            parts[l][0].n_loads = len(att_loads(l, parts[l][0]))
        N_FIRST = len(first_loads) + 4

        block = ctx.enter_context(nc.Block())

        @block.sync
        def _(sp):
            sp.dma_start(x[:, :].rearrange("s (b d) -> s b d", b=B), a["x"].rearrange("b s d -> s b d")).then_inc(loaded, 16)
            for dst, name in first_loads:
                sp.dma_start(dst[:, :], a[name]).then_inc(loaded, 16)
            sp.dma_start(gb[:, :], a["gb"].to_broadcast([128, E])).then_inc(loaded, 16)
            for l in range(2):
                sp.dma_start(bo[l][:, :], a[f"bo{l}"].to_broadcast([128, D])).then_inc(loaded, 16)
            for l, (A, X) in enumerate(parts):
                if l:
                    sp.wait_ge(phase, 2)
                for dst, src in att_loads(l, A):
                    sp.dma_start(dst, src).then_inc(A.w_loaded, 16)
                sp.wait_ge(phase, 2 * l + 1)
                route_sync(sp, l)
                ffn_sync(sp, X, {"in": a["w1_0"], "out": a["w2_0"], "bias": a["b1"]} if l == 0 else
                         {"in": a["w1_1"], "up": a["w2_1"], "out": a["w3_1"]}, l)
            sp.wait_ge(phase, 4)
            sp.dma_start(out.rearrange("b s d -> s b d"), x[:, :].rearrange("s (b d) -> s b d", b=B)).then_inc(finished, 16)
            sp.wait_ge(finished, 16)

        @block.tensor
        def _(pe):
            pe.wait_ge(loaded, 16 * N_FIRST)
            for l, (A, X) in enumerate(parts):
                norm_tensor(pe, 2 * l)
                if l == 0:
                    pe.wait_ge(ctx_split, 1)
                pe.wait_ge(xt_ready, NGROUP * (2 * l + 1))
                att_tensor(pe, A)
                pe.wait_ge(phase, 2 * l + 1)
                norm_tensor(pe, 2 * l + 1)
                route_tensor(pe, l)
                pe.wait_ge(xt_ready, NGROUP * (2 * l + 2))
                ffn_tensor(pe, X)
                pe.wait_ge(phase, 2 * l + 2)

        @block.scalar
        def _(act):
            act.wait_ge(loaded, 16 * N_FIRST)
            for l, (A, X) in enumerate(parts):
                norm_scalar(act, 2 * l)
                act.wait_ge(phase, 2 * l) if l else None
                att_scalar(act, A)
                act.wait_ge(phase, 2 * l + 1)
                norm_scalar(act, 2 * l + 1)
                route_scalar(act, l)
                ffn_scalar(act, X)
                act.wait_ge(phase, 2 * l + 2)

        @block.gpsimd
        def _(p):
            p.memset(zeros[:, :], 0.0).then_inc(pool_own, 1)
            p.wait_ge(loaded, 16 * N_FIRST)
            for l, (A, X) in enumerate(parts):
                norm_pool(p, 2 * l)
                p.wait_ge(xn_ready, B * (2 * l + 1))
                xv = x[:, :].rearrange("p (b d) -> p b d", b=B)
                bb = bo[l][:, :].rearrange("p (o d) -> p o d", o=1).to_broadcast([128, B, D])
                p.tensor_tensor(xv, xv, bb, ALU.add).then_inc(bo_ready, 1)
                att_pool(p, A)
                p.wait_ge(phase, 2 * l + 1)
                norm_pool(p, 2 * l + 1)
                ffn_pool(p, X)
                p.wait_ge(phase, 2 * l + 2)

        @block.vector
        def _(v):
            v.wait_ge(loaded, 16 * N_FIRST)
            k = seq(v.tensor_copy(ct_hi[:, :], ct[:, :]))
            v.wait_ge(dve, k)
            v.tensor_tensor(ct_lo[:, :], ct[:, :], ct_hi[:, :].bitcast(F32), ALU.subtract).then_inc(ctx_split, 1)
            for l, (A, X) in enumerate(parts):
                norm_vector(v, 2 * l)
                v.wait_ge(bo_ready, l + 1)
                att_vector(v, A)
                norm_vector(v, 2 * l + 1)
                route_vector(v, l)
                ffn_vector(v, X)


def kernel(**inputs):
    import concourse.bacc as bacc
    from concourse.bass_utils import run_bass_kernel_spmd

    f = {n: np.asarray(v) for n, v in inputs.items()}
    rows = np.arange(128)
    copy_no, head_no = rows // 32, (rows % 32) // HD0
    masks = np.stack([copy_no >= 2, copy_no % 2 == 1] + [head_no == j for j in range(4)], axis=1)

    def replicated(w):
        wt = w.T.reshape(D, QUADS, 1, 32)
        return np.broadcast_to(wt, (D, QUADS, 4, 32)).reshape(D, QUADS * 128)

    def replicated_bias(b):
        bt = b.reshape(QUADS, 1, 32)
        return np.broadcast_to(bt, (QUADS, 4, 32)).reshape(QUADS, 128).T

    def chunks(w, width):
        e, hid, o = w.shape
        whole = np.zeros((e, width, o), w.dtype)
        whole[:, :hid] = w
        return whole.reshape(e, width // 128, 128, o).transpose(0, 2, 1, 3).reshape(e * 128, -1)

    wo0 = np.zeros((QUADS, 4, 32, D), f["L0_xattn_Wo"].dtype)
    wo0[:, :, :HD0] = f["L0_xattn_Wo"].T.reshape(QUADS, 4, HD0, D)
    arrays = {
        "x": f["x"],
        "ct": f["ctx_1024"].reshape(TOK, D).T,
        "masks": masks.astype(np.float32),
        "ident": np.eye(128, dtype=np.float32),
        "minus_half": np.full((128, B), -0.5, np.float32),
        "expert_no": np.broadcast_to(np.repeat(np.arange(E, dtype=np.float32), B), (128, E * B)),
        "wq0": replicated(f["L0_xattn_Wq"]), "wk0": replicated(f["L0_xattn_Wk"]),
        "wv0": f["L0_xattn_Wv"].T,
        "wo0": wo0.reshape(QUADS, 128, D).transpose(1, 0, 2).reshape(128, QUADS * D),
        "bq": replicated_bias(f["L0_xattn_bq"]), "bk": replicated_bias(f["L0_xattn_bk"]),
        "bv": f["L0_xattn_bv"].reshape(1, D),
        "bo0": f["L0_xattn_bo"].reshape(1, D), "bo1": f["L1_xattn_bo"].reshape(1, D),
        "gw0": f["L0_ffn_gate_w"], "gb": f["L0_ffn_gate_b"].reshape(1, E),
        "w1_0": np.concatenate([f["L0_ffn_w1"], f["L0_ffn_ws1"][None]]).reshape(E0 * 128, HID0),
        "w2_0": chunks(np.concatenate([f["L0_ffn_w2"], f["L0_ffn_ws2"][None]]), HID0),
        "b1": np.concatenate([f["L0_ffn_b1"], f["L0_ffn_bs1"][None]]).reshape(E0, JOBS0, 128).transpose(0, 2, 1).reshape(E0 * 128, JOBS0),
        "b2": np.concatenate([f["L0_ffn_b2"], f["L0_ffn_bs2"][None]]).T,
        "wq1": f["L1_xattn_Wq"], "wk1": f["L1_xattn_Wk"], "wv1": f["L1_xattn_Wv"],
        "wo1": f["L1_xattn_Wo"].reshape(8, 128, D).transpose(1, 0, 2).reshape(128, 8 * D),
        "gw1": f["L1_ffn_Wg"].T,
        "w1_1": f["L1_ffn_W1"].transpose(0, 2, 1).reshape(E * 128, HID1),
        "w2_1": f["L1_ffn_W2"].transpose(0, 2, 1).reshape(E * 128, HID1),
        "w3_1": chunks(f["L1_ffn_W3"].transpose(0, 2, 1), JOBS1 * 128),
    }
    nc = bacc.Bacc("TRN2", target_bir_lowering=False, num_devices=1)
    named, aps = {}, {}
    for name, value in arrays.items():
        value = np.ascontiguousarray(value)
        named["in_" + name] = value
        aps[name] = nc.dram_tensor("in_" + name, value.shape, mybir.dt.from_np(value.dtype), kind="ExternalInput").ap()
    result = nc.dram_tensor("result", (B, S, D), F32, kind="ExternalOutput").ap()
    build(nc, aps, result)
    r = run_bass_kernel_spmd(nc, [named], core_ids=[0])
    return r.results[0]["result"]
```

```python
from contextlib import ExitStack

import numpy as np

import concourse.bass as bass
from concourse import mybir

F32 = mybir.dt.float32
F32R = mybir.dt.float32r
U32 = mybir.dt.uint32
ALU = mybir.AluOpType
ACT = mybir.ActivationFunctionType
AX_X = mybir.AxisListType.X

B, S, D = 16, 128, 128
TOK = B * S
H = 16
HD0, HD1 = 8, 64
INNER1 = H * HD1
E = 8
HID0, HID1 = 512, 352
E0 = E + 1
EPS = 1e-5

GROUP = 512
NGROUP = TOK // GROUP
BPG = GROUP // S
QUADS = H // 4
UNITS = QUADS * BPG
SCALE0 = 1.0 / (D / H) ** 0.5
SCALE1 = HD1 ** -0.5
JOBS0 = HID0 // 128
JOBS1 = -(-HID1 // 128)
RING = 4
SLOTS = 6



def span(start, size):
    return slice(start, start + size) if isinstance(start, int) else bass.ds(start, size)


def until(eng, sem, value):
    if not isinstance(value, int) or value > 0:
        eng.wait_ge(sem, value)


def side_jobs(layer):
    at = {-1: [("V", b) for b in range(BPG)]}
    for n in range(NGROUP * UNITS):
        g, u = divmod(n, UNITS)
        at[n] = []
        if layer == 0:
            if u >= 14 and g < NGROUP - 1:
                at[n].append(("V", BPG * (g + 1) + u - 14))
            if u <= 1 and g:
                at[n].append(("V", BPG * g + u + 2))
            batches = [u - 3] if 3 <= u < 3 + BPG else []
        else:
            if 1 <= n < NGROUP * UNITS - 3:
                at[n].append(("V", n + 3))
            batches = [u - 1] if 1 <= u <= BPG else []
        if g:
            at[n] += [("O", BPG * (g - 1) + b) for b in batches]
    at[NGROUP * UNITS] = [("O", BPG * (NGROUP - 1) + b) for b in range(BPG)]
    return at


def build(nc, a, out):
    c_dram = nc.dram_tensor("gates_by_expert", [2, E, TOK], F32, kind="Internal").ap()

    with ExitStack() as ctx:
        def sb(name, shape, dt=F32, stack=ctx):
            return stack.enter_context(nc.sbuf_tensor(name, shape, dt))

        def sem(name):
            return ctx.enter_context(nc.semaphore(name))

        bank = [ctx.enter_context(nc.psum_tensor(f"bank{i}", [128, GROUP], F32)) for i in range(8)]

        x = sb("x", [128, TOK])
        xn = sb("xn", [128, TOK])
        xt = sb("xt", [128, TOK])
        xt_hi = sb("xt_hi", [128, TOK], F32R)
        xt_lo = sb("xt_lo", [128, TOK], F32R)
        ct = sb("ct", [128, TOK])
        ct_hi = sb("ct_hi", [128, TOK], F32R)
        ct_lo = sb("ct_lo", [128, TOK], F32R)
        y = sb("y", [128, TOK])
        ident = sb("ident", [128, 128])
        expert_no = sb("expert_no", [128, E * B])
        masks = sb("masks", [128, 6])
        stats = sb("stats", [128, B * 6])
        meanvar = sb("meanvar", [128, B * 2])
        veps = sb("veps", [128, B])
        minus_half = sb("minus_half", [128, B])
        rstd = sb("rstd", [128, B])
        gw = [sb(f"gw{l}", [128, E]) for l in range(2)]
        gb = sb("gb", [128, E])
        logit = sb("logit", [128, B * E])
        top = sb("top", [128, B * 8])
        topi = sb("topi", [128, B * 8], U32)
        topf = sb("topf", [128, B * 2])
        gdiff = sb("gdiff", [128, B])
        gexp = sb("gexp", [128, B])
        gone = sb("gone", [128, B])
        gweight = sb("gweight", [128, 2 * B])
        hot1 = sb("hot1", [128, E * B])
        hot2 = sb("hot2", [128, E * B])
        combine = sb("combine", [128, E * B])
        combine_t = sb("combine_t", [128, 128])
        zeros = sb("zeros", [128, HID0])
        b2 = sb("b2", [128, E0])
        bo = [sb(f"bo{l}", [128, D]) for l in range(2)]
        negmax = sb("negmax", [128, SLOTS * 4])
        total = sb("total", [128, SLOTS * 4])
        rtotal = sb("rtotal", [128, SLOTS * 4])

        loaded = sem("loaded")
        ctx_split = sem("ctx_split")
        dve = sem("dve")
        pow_done = sem("pow_done")
        norm_in = sem("norm_in")
        xn_ready = sem("xn_ready")
        xt_ps = sem("xt_ps")
        xt_copied = sem("xt_copied")
        xt_ready = sem("xt_ready")
        bias_added = sem("bias_added")
        phase = sem("phase")
        table_ready = sem("table_ready")

        dve_n = [0]

        def seq(ins):
            dve_n[0] += 1
            ins.then_inc(dve, 1)
            return dve_n[0]

        def norm_vector(v, n):
            for t in range(B):
                k = seq(v.bn_stats(stats[:, t * 6:t * 6 + 6], x[:, t * D:(t + 1) * D]))
            v.wait_ge(dve, k)
            for t in range(B):
                k = seq(v.bn_aggr(meanvar[:, 2 * t:2 * t + 2], stats[:, t * 6:t * 6 + 6]))
            v.wait_ge(dve, k)
            var = meanvar[:, :].rearrange("p (t k) -> p t k", k=2)[:, :, 1]
            v.tensor_scalar(veps[:, :], var, EPS, None, ALU.add).then_inc(norm_in, 1)
            v.wait_ge(pow_done, n + 1)
            for t in range(B):
                v.tensor_scalar(xn[:, t * D:(t + 1) * D], x[:, t * D:(t + 1) * D],
                                meanvar[:, 2 * t:2 * t + 1], rstd[:, t:t + 1],
                                ALU.subtract, ALU.mult).then_inc(xn_ready, 1)
            for g in range(NGROUP):
                cols = slice(g * GROUP, (g + 1) * GROUP)
                v.wait_ge(xt_copied, NGROUP * n + g + 1)
                k = seq(v.tensor_copy(xt_hi[:, cols], xt[:, cols]))
                v.wait_ge(dve, k)
                v.tensor_tensor(xt_lo[:, cols], xt[:, cols], xt_hi[:, cols].bitcast(F32),
                                ALU.subtract).then_inc(xt_ready, 1)

        def norm_pool(p, n):
            p.wait_ge(norm_in, n + 1)
            p.tensor_tensor(rstd[:, :], veps[:, :], minus_half[:, :], ALU.pow).then_inc(pow_done, 1)

        def norm_tensor(pe, n):
            for g in range(NGROUP):
                if g >= 2:
                    pe.wait_ge(xt_copied, NGROUP * n + g - 1)
                for b in range(BPG):
                    t = g * BPG + b
                    pe.wait_ge(xn_ready, B * n + t + 1)
                    ins = pe.transpose(bank[g % 2][:, b * 128:(b + 1) * 128], xn[:, t * D:(t + 1) * D], ident[:, :])
                ins.then_inc(xt_ps, 1)

        def norm_scalar(act, n):
            for g in range(NGROUP):
                act.wait_ge(xt_ps, NGROUP * n + g + 1)
                act.activation(xt[:, g * GROUP:(g + 1) * GROUP], bank[g % 2][:, :], ACT.Copy).then_inc(xt_copied, 1)

        class Attention:

            def __init__(self, l, stack):
                self.l = l
                n = f"{l}"
                s = lambda name: sem(name + n)
                self.w_loaded, self.w_split = s("w_loaded"), s("w_split")
                self.qk_ps, self.qk_copied = s("qk_ps"), s("qk_copied")
                self.side_ps, self.side_done = s("side_ps"), s("side_done")
                self.scored, self.maxed, self.exped = s("scored"), s("maxed"), s("exped")
                self.inverted, self.normed = s("inverted"), s("normed")
                self.turned, self.turned_a, self.turned_v = s("turned"), s("turned_a"), s("turned_v")
                self.weighed, self.out_copied = s("weighed"), s("out_copied")
                self.cleared = s("cleared")
                self.halved, self.k_rest, self.k_ready, self.q_ready = s("halved"), s("k_rest"), s("k_ready"), s("q_ready")
                self.cols = QUADS * 128 if l == 0 else INNER1
                b_ = lambda name, shape, dt=F32: sb(name + n, shape, dt, stack)
                self.names = ("q", "k") if l == 0 else ("q", "k", "v")
                self.raw = {w: b_("raw_" + w, [128, self.cols]) for w in self.names}
                self.hi = {w: b_("hi_" + w, [128, self.cols], F32R) for w in self.names}
                self.lo = {w: b_("lo_" + w, [128, self.cols], F32R) for w in self.names}
                self.p = [b_(f"p{i}_", [128, 512]) for i in range(SLOTS)]
                self.pt = [b_(f"pt{i}_", [128, 512]) for i in range(2)]
                if l == 0:
                    self.wv, self.wo = b_("wv", [128, D]), b_("wo", [128, QUADS * D])
                    self.bq, self.bk, self.bv = b_("bq", [128, QUADS]), b_("bk", [128, QUADS]), b_("bv", [128, D])
                    self.bqs = b_("bqs", [128, QUADS])
                    self.q = [b_(f"q{i}_", [128, GROUP], F32R) for i in range(2)]
                    self.k = [b_(f"k{i}_", [128, BPG * 4 * S], F32R) for i in range(2)]
                    self.full = {w: b_("full" + w, [128, GROUP]) for w in "qk"}
                    self.half = {w: b_("half" + w, [128, GROUP], F32R) for w in "qk"}
                    self.kst = b_("kst", [128, GROUP], F32R)
                    self.v = b_("v", [128, BPG * H * 32])
                    self.ot = b_("ot", [128, QUADS * GROUP])
                else:
                    self.wo = b_("wo", [128, 8 * D])
                    self.q = [b_(f"q{i}_", [128, 2 * GROUP]) for i in range(2)]
                    self.k = [b_(f"k{i}_", [128, 2 * BPG * 2 * S]) for i in range(2)]
                    self.v = [b_(f"v{i}_", [128, BPG * 256]) for i in range(2)]
                    self.ot = b_("ot", [128, 8 * GROUP])
                self.qk_jobs = 2 if l == 0 else 4
                self.side_at = side_jobs(l)
                self.side_place = {}
                for n_ in sorted(self.side_at):
                    for job in self.side_at[n_]:
                        self.side_place[job] = len(self.side_place)
                self.out_per = 4 if l == 0 else 2

            def qk_at(self, n):
                block, job = divmod(n + (11 if self.l == 0 else 9), 4)
                return [(block, job)] if job < self.qk_jobs and 2 <= block < QUADS * NGROUP else []

        NU = NGROUP * UNITS

        def three(pe, ps, w_hi, w_lo, m_hi, m_lo):
            pe.matmul(ps, w_lo, m_hi, start=True, stop=False)
            pe.matmul(ps, w_hi, m_lo, start=False, stop=False)
            return pe.matmul(ps, w_hi, m_hi, start=False, stop=True)

        def att_tensor(pe, A):
            l = A.l
            qk_bank = bank[6]

            def qk_job(block, job):
                g, quad = divmod(block, QUADS)
                until(pe, A.qk_copied, A.qk_jobs * block + job)
                if l == 0:
                    w, at = "kq"[job], quad * 128
                else:
                    w, at = "qk"[job // 2], (2 * quad + job % 2) * 128
                hi, lo = (xt_hi, xt_lo) if w == "q" else (ct_hi, ct_lo)
                m = slice(g * GROUP, (g + 1) * GROUP)
                three(pe, qk_bank[:, :], A.hi[w][:, at:at + 128], A.lo[w][:, at:at + 128],
                      hi[:, m], lo[:, m]).then_inc(A.qk_ps, 1)

            def side_job(name, item):
                until(pe, A.side_done, A.side_place[name, item])
                side_ps = bank[7][:, 0:D if name == "O" or l == 0 else 256]
                if name == "V" and l == 0:
                    t = item
                    ins = pe.matmul(side_ps, ct[:, t * S:(t + 1) * S], A.wv[:, :], start=True, stop=True)
                elif name == "V":
                    g, u = divmod(item, UNITS)
                    quad, b = divmod(u, BPG)
                    t = g * BPG + b
                    c, w = slice(t * S, (t + 1) * S), slice(quad * 256, (quad + 1) * 256)
                    ins = three(pe, side_ps, ct_hi[:, c], ct_lo[:, c], A.hi["v"][:, w], A.lo["v"][:, w])
                else:
                    g, b = divmod(item, BPG)
                    pe.wait_ge(A.out_copied, (g + 1) * UNITS // A.out_per - (1 if l and b < 2 else 0))
                    parts = QUADS if l == 0 else 8
                    for i in range(parts):
                        ins = pe.matmul(side_ps, A.ot[:, i * GROUP + b * S:i * GROUP + (b + 1) * S],
                                        A.wo[:, i * D:(i + 1) * D], start=(i == 0), stop=(i == parts - 1))
                ins.then_inc(A.side_ps, 1)

            def score(n):
                block, b = divmod(n, BPG)
                q, k = A.q[block % 2], A.k[block % 2]
                ps = bank[n % 2]
                if l == 0:
                    pe.wait_ge(A.k_ready, block + 1)
                    pe.wait_ge(A.q_ready, block + 1)
                else:
                    pe.wait_ge(A.qk_copied, 4 * (block + 1))
                until(pe, A.exped, n - 1)
                if l == 0:
                    ins = pe.matmul(ps[:, :], q[:, b * S:(b + 1) * S], k[:, b * 512:(b + 1) * 512],
                                    start=True, stop=True)
                else:
                    for pair in range(2):
                        at = (pair * BPG + b) * 256
                        ins = pe.matmul(ps[:, pair * 256:(pair + 1) * 256],
                                        q[:, pair * GROUP + b * S:pair * GROUP + (b + 1) * S],
                                        k[:, at:at + 256], start=True, stop=True)
                ins.then_inc(A.scored, 1)

            def turn(n):
                pe.wait_ge(A.normed, n + 1)
                until(pe, A.turned_v if n % 2 else A.turned_a, n // 2)
                for j in range(4):
                    ins = pe.transpose(bank[2 + n % 2][:, j * 128:(j + 1) * 128],
                                       A.p[n % SLOTS][:, j * 128:(j + 1) * 128], ident[:, :])
                ins.then_inc(A.turned, 1)

            def weigh(n):
                block, b = divmod(n, BPG)
                quad = block % QUADS
                g = n // UNITS
                pe.wait_ge(A.turned_v if n % 2 else A.turned_a, n // 2 + 1)
                chunk = n // A.out_per
                ps = bank[4 + chunk % 2]
                if n % A.out_per == 0:
                    until(pe, A.out_copied, chunk - 1)
                v_item = BPG * g + b if l == 0 else n
                pe.wait_ge(A.side_done, A.side_place["V", v_item] + 1)
                pt = A.pt[n % 2]
                for j in range(4):
                    if l == 0:
                        at = (b * H + 4 * quad + j) * 32
                        ins = pe.matmul(ps[32 * j:32 * j + 32, b * 128:(b + 1) * 128], A.v[:, at:at + 32],
                                        pt[:, j * 128:(j + 1) * 128], start=True, stop=True)
                    else:
                        pair, half = divmod(j, 2)
                        at = b * 256 + j * 64
                        col = pair * 256 + (b % 2) * 128
                        ins = pe.matmul(ps[64 * half:64 * half + 64, col:col + 128],
                                        A.v[block % 2][:, at:at + 64],
                                        pt[:, j * 128:(j + 1) * 128], start=True, stop=True)
                ins.then_inc(A.weighed, 1)

            pe.wait_ge(A.w_split, len(A.names))
            pe.wait_ge(A.w_loaded, 16 * A.n_loads)
            for block in range(2):
                for job in range(A.qk_jobs):
                    qk_job(block, job)
                if block == 0:
                    for job in A.side_at[-1]:
                        side_job(*job)
            for n in (-3, -2):
                for job in A.qk_at(n):
                    qk_job(*job)
            for n in range(4):
                score(n)
            for job in A.qk_at(-1):
                qk_job(*job)
            for n in range(NU + 2):
                if n + 4 < NU:
                    score(n + 4)
                if n < NU:
                    turn(n)
                    for job in A.qk_at(n):
                        qk_job(*job)
                    for job in A.side_at[n]:
                        side_job(*job)
                if n >= 2:
                    weigh(n - 2)
            for job in A.side_at[NU]:
                side_job(*job)

        def att_scalar(act, A):
            l = A.l

            def exps(n):
                act.wait_ge(A.maxed, n + 1)
                until(act, A.turned, n - SLOTS + 1)
                until(act, A.inverted, n - SLOTS + 1)
                for j in range(4):
                    col = (n % SLOTS) * 4 + j
                    ins = act.activation(A.p[n % SLOTS][:, j * 128:(j + 1) * 128],
                                         bank[n % 2][:, j * 128:(j + 1) * 128], ACT.Exp,
                                         bias=negmax[:, col:col + 1], scale=1.0, accum_out=total[:, col:col + 1])
                ins.then_inc(A.exped, 1)

            def copy_out(n):
                act.wait_ge(A.turned, n + 1)
                until(act, A.weighed, n - 1)
                act.activation(A.pt[n % 2][:, :], bank[2 + n % 2][:, :], ACT.Copy).then_inc(A.turned_a, 1)

            def qk_copy(block, job):
                quad = block % QUADS
                act.wait_ge(A.qk_ps, A.qk_jobs * block + job + 1)
                if l == 0:
                    w = "kq"[job]
                    until(act, A.q_ready if w == "q" else A.k_rest, block)
                    act.activation(A.full[w][:, :], bank[6][:, :], ACT.Identity,
                                   bias=(A.bqs if w == "q" else A.bk)[:, quad:quad + 1],
                                   scale=SCALE0 if w == "q" else 1.0).then_inc(A.qk_copied, 1)
                    return
                until(act, A.scored, BPG * (block - 1))
                pair = job % 2
                if job < 2:
                    act.activation(A.q[block % 2][:, pair * GROUP:(pair + 1) * GROUP], bank[6][:, :], ACT.Copy,
                                   scale=SCALE1).then_inc(A.qk_copied, 1)
                    return
                k = A.k[block % 2][:, pair * 1024:(pair + 1) * 1024].rearrange("p (b h s) -> p b h s", b=BPG, h=2)
                ps = bank[6][:, :].rearrange("p (b s) -> p b s", b=BPG)
                if block < 2:
                    act.wait_ge(A.cleared, 1 + block)
                act.activation(k[0:64, :, 0, :], ps[0:64], ACT.Copy)
                act.activation(k[64:128, :, 1, :], ps[64:128], ACT.Copy).then_inc(A.qk_copied, 1)

            if l == 0:
                act.wait_ge(A.cleared, 2)
            for block in range(2):
                for job in range(A.qk_jobs):
                    qk_copy(block, job)
            for n in (-3, -2):
                for job in A.qk_at(n):
                    qk_copy(*job)
            for n in range(3):
                exps(n)
            for n in range(NU + 1):
                for job in A.qk_at(n - 1):
                    qk_copy(*job)
                if n + 3 < NU:
                    exps(n + 3)
                if n and (n - 1) % 2 == 0:
                    copy_out(n - 1)

        def att_pool(p, A):
            if A.l == 0:
                p.memset(A.v[:, :], 0.0).then_inc(A.cleared, 1)
            else:
                for i in range(2):
                    p.memset(A.k[i][:, :], 0.0).then_inc(A.cleared, 1)
            for w in A.names:
                p.wait_ge(A.w_loaded, 16 * A.n_loads)
                p.tensor_copy(A.hi[w][:, :], A.raw[w][:, :]).then_inc(pool_own, 1)
                pool_n[0] += 1
                p.wait_ge(pool_own, pool_n[0])
                p.tensor_tensor(A.lo[w][:, :], A.raw[w][:, :], A.hi[w][:, :].bitcast(F32),
                                ALU.subtract).then_inc(A.w_split, 1)

            def rest(block, job):
                w = "kq"[job]
                p.wait_ge(A.halved, 2 * block + job + 1)
                if w == "k":
                    until(p, A.k_ready, block)
                else:
                    until(p, A.scored, BPG * (block - 1))
                p.tensor_tensor((A.kst if w == "k" else A.q[block % 2])[:, :], A.full[w][:, :],
                                A.half[w][:, :].bitcast(F32), ALU.subtract
                                ).then_inc(A.k_rest if w == "k" else A.q_ready, 1)

            if A.l == 0:
                for block in range(2):
                    for job in range(2):
                        rest(block, job)
            for n in range(NU):
                s = (n % SLOTS) * 4
                p.wait_ge(A.inverted, n + 1)
                pr = A.p[n % SLOTS][:, :].rearrange("p (h s) -> p h s", h=4)
                p.tensor_tensor(pr, pr, rtotal[:, s:s + 4].rearrange("p (h o) -> p h o", o=1).to_broadcast([128, 4, 128]),
                                ALU.mult).then_inc(A.normed, 1)
                if A.l == 0 and n % 4 in (1, 2) and n // 4 + 2 < QUADS * NGROUP:
                    rest(n // 4 + 2, n % 4 - 1)

        def att_vector(v, A):
            l = A.l

            def row_max(n):
                v.wait_ge(A.scored, n + 1)
                until(v, A.exped, n - SLOTS + 1)
                s = (n % SLOTS) * 4
                v.tensor_reduce(negmax[:, s:s + 4], bank[n % 2][:, :].rearrange("p (h s) -> p h s", h=4),
                                AX_X, ALU.max, negate=True).then_inc(A.maxed, 1)

            def invert(n):
                v.wait_ge(A.exped, n + 1)
                until(v, A.normed, n - SLOTS + 1)
                s = (n % SLOTS) * 4
                v.reciprocal(rtotal[:, s:s + 4], total[:, s:s + 4]).then_inc(A.inverted, 1)

            def copy_out(n):
                v.wait_ge(A.turned, n + 1)
                until(v, A.weighed, n - 1)
                v.tensor_copy(A.pt[n % 2][:, :], bank[2 + n % 2][:, :]).then_inc(A.turned_v, 1)

            def out_copy(chunk):
                v.wait_ge(A.weighed, A.out_per * (chunk + 1))
                g, c = divmod(chunk, UNITS // A.out_per)
                if g:
                    batches = BPG if l == 0 or c % 2 else 2
                    if c < (1 if l == 0 else 2):
                        v.wait_ge(A.side_ps, A.side_place["O", BPG * (g - 1) + batches - 1] + 1)
                ps = bank[4 + chunk % 2]
                if l == 0:
                    v.tensor_copy(A.ot[:, c * GROUP:(c + 1) * GROUP], ps[:, :]).then_inc(A.out_copied, 1)
                else:
                    quad, half = divmod(c, 2)
                    o = A.ot[:, 2 * quad * GROUP:(2 * quad + 2) * GROUP].rearrange("p (i s) -> p i s", i=2)
                    v.tensor_copy(o[:, :, half * 256:(half + 1) * 256],
                                  ps[:, :].rearrange("p (i s) -> p i s", i=2)).then_inc(A.out_copied, 1)

            def half(block, job):
                w = "kq"[job]
                v.wait_ge(A.qk_copied, 2 * block + job + 1)
                until(v, A.q_ready if w == "q" else A.k_rest, block)
                low_rows = masks[:, 0:1] if w == "q" else masks[:, 1:2]
                v.tensor_scalar(A.half[w][:, :], A.full[w][:, :], low_rows, None, ALU.mult).then_inc(A.halved, 1)

            def head_keys(block, heads):
                v.wait_ge(A.k_rest, block + 1)
                until(v, A.scored, BPG * (block - 1))
                kk = A.k[block % 2][:, :].rearrange("p (b h s) -> p b h s", b=BPG, h=4)
                for j in heads:
                    ins = v.tensor_scalar(kk[:, :, j, :], A.kst[:, :].bitcast(F32).rearrange("p (b s) -> p b s", b=BPG),
                                          masks[:, 2 + j:3 + j], None, ALU.mult)
                if heads[-1] == 3:
                    ins.then_inc(A.k_ready, 1)

            def side(name, item):
                v.wait_ge(A.side_ps, A.side_place[name, item] + 1)
                side_ps = bank[7][:, 0:D if name == "O" or l == 0 else 256]
                if name == "V" and l == 0:
                    b = item % BPG
                    until(v, A.weighed, UNITS * (item // BPG) - BPG + b + 1 if item >= BPG else 0)
                    if item < BPG:
                        v.wait_ge(A.cleared, 1)
                    vv = A.v[:, b * 512:(b + 1) * 512].rearrange("p (h c) -> p h c", h=H)[:, :, 0:HD0]
                    v.tensor_tensor(vv, side_ps.rearrange("p (h c) -> p h c", h=H),
                                    A.bv[:, :].rearrange("p (h c) -> p h c", h=H), ALU.add).then_inc(A.side_done, 1)
                elif name == "V":
                    block, b = divmod(item, BPG)
                    until(v, A.weighed, item - 8 + 1)
                    v.tensor_copy(A.v[block % 2][:, b * 256:(b + 1) * 256], side_ps).then_inc(A.side_done, 1)
                else:
                    t = item
                    xs = x[:, t * D:(t + 1) * D]
                    v.tensor_tensor(xs, side_ps, xs, ALU.add).then_inc(A.side_done, 1)

            if l == 0:
                v.wait_ge(A.w_loaded, 16 * A.n_loads)
                v.tensor_scalar(A.bqs[:, :], A.bq[:, :], SCALE0, None, ALU.mult).then_inc(A.cleared, 1)
                for block in range(2):
                    for job in range(2):
                        half(block, job)
                    head_keys(block, (0, 1, 2, 3))
                    if block == 0:
                        for job in A.side_at[-1]:
                            side(*job)
                half(2, 0)
            else:
                for job in A.side_at[-1]:
                    side(*job)
            for n in range(4):
                row_max(n)
            for n in range(2):
                invert(n)
            for n in range(NU + 3):
                if 0 < n <= NU:
                    for job in A.side_at[n - 1]:
                        side(*job)
                if n + 2 < NU:
                    invert(n + 2)
                if n <= NU and n and (n - 1) % 2:
                    copy_out(n - 1)
                if n + 4 < NU:
                    row_max(n + 4)
                if l == 0:
                    for block in range(2, QUADS * NGROUP):
                        r = n - 4 * block
                        if r in (-9, -8):
                            half(block, r + 9)
                        if r in (-6, -5):
                            head_keys(block, (0, 1) if r == -6 else (2, 3))
                if n > 2 and (n - 2) % A.out_per == 0:
                    out_copy((n - 2) // A.out_per - 1)
            for job in A.side_at[NU]:
                side(*job)
            v.wait_ge(A.side_done, len(A.side_place))
            v.sem_inc(phase, 1)

        router = {n: sem("router_" + n) for n in ("logits", "max", "exp", "ready", "turned", "copied", "stored")}

        def route_tensor(pe, l):
            pe.wait_ge(xt_copied, NGROUP * (2 * l + 2))
            for t in range(B):
                ins = pe.matmul(bank[6][:, t * E:(t + 1) * E], xt[:, t * S:(t + 1) * S], gw[l][:, :],
                                start=True, stop=True)
            ins.then_inc(router["logits"], 1)
            pe.wait_ge(router["ready"], l + 1)
            pe.transpose(bank[7][:, 0:128], combine[:, :], ident[:, :]).then_inc(router["turned"], 1)

        def route_vector(v, l):
            v.wait_ge(router["logits"], l + 1)
            lg = logit[:, :].rearrange("p (t e) -> p t e", e=E)
            ps = bank[6][:, 0:B * E].rearrange("p (t e) -> p t e", e=E)
            if l == 0:
                gbb = gb[:, :].rearrange("p (o e) -> p o e", o=1).to_broadcast([128, B, E])
                k = seq(v.tensor_tensor(lg, ps, gbb, ALU.add))
            else:
                k = seq(v.tensor_copy(lg, ps))
            v.wait_ge(dve, k)
            for t in range(B):
                k = seq(v.max(top[:, t * 8:(t + 1) * 8], logit[:, t * E:(t + 1) * E]))
            v.wait_ge(dve, k)
            for t in range(B):
                k = seq(v.max_index(topi[:, t * 8:(t + 1) * 8], top[:, t * 8:(t + 1) * 8],
                                    logit[:, t * E:(t + 1) * E]))
            v.wait_ge(dve, k)
            tops = top[:, :].rearrange("p (t k) -> p t k", k=8)
            two = lambda buf: buf[:, :].rearrange("p (t k) -> p t k", k=2)
            k = seq(v.tensor_copy(two(topf), topi[:, :].rearrange("p (t k) -> p t k", k=8)[:, :, 0:2]))
            w = two(gweight)
            if l == 0:
                k = seq(v.tensor_tensor(gdiff[:, :], tops[:, :, 1], tops[:, :, 0], ALU.subtract))
                v.wait_ge(dve, k)
                v.sem_inc(router["max"], 1)
                v.wait_ge(router["exp"], 1)
                k = seq(v.tensor_scalar(gone[:, :], gexp[:, :], 1.0, None, ALU.add))
                v.wait_ge(dve, k)
                k = seq(v.reciprocal(w[:, :, 0], gone[:, :]))
                v.wait_ge(dve, k)
                k = seq(v.tensor_tensor(w[:, :, 1], gexp[:, :], w[:, :, 0], ALU.mult))
            else:
                k = seq(v.tensor_copy(w, tops[:, :, 0:2]))
            v.wait_ge(dve, k)
            no = expert_no[:, :].rearrange("p (e t) -> p e t", t=B)
            col = lambda buf, i: two(buf)[:, :, i].rearrange("p (o t) -> p o t", o=1).to_broadcast([128, E, B])
            hots = [hot1[:, :].rearrange("p (e t) -> p e t", t=B), hot2[:, :].rearrange("p (e t) -> p e t", t=B)]
            for i in range(2):
                k = seq(v.tensor_tensor(hots[i], no, col(topf, i), ALU.is_equal))
            v.wait_ge(dve, k)
            for i in range(2):
                k = seq(v.tensor_tensor(hots[i], hots[i], col(gweight, i), ALU.mult))
            v.wait_ge(dve, k)
            v.tensor_tensor(combine[:, :], hot1[:, :], hot2[:, :], ALU.add).then_inc(router["ready"], 1)
            v.wait_ge(router["turned"], l + 1)
            v.tensor_copy(combine_t[:, :], bank[7][:, 0:128]).then_inc(router["copied"], 1)

        def route_scalar(act, l):
            if l == 0:
                act.wait_ge(router["max"], 1)
                act.activation(gexp[:, :], gdiff[:, :], ACT.Exp).then_inc(router["exp"], 1)

        def route_sync(sp, l):
            sp.wait_ge(router["copied"], l + 1)
            sp.dma_start(c_dram[l].rearrange("e (t s) -> (e t) s", t=B), combine_t[:, :]).then_inc(router["stored"], 16)
            sp.wait_ge(router["stored"], 16 * (l + 1))

        LAG = 3

        class Experts:
            def __init__(self, l, stack):
                self.l = l
                n = f"_x{l}"
                s = lambda name: sem(name + n)
                self.n = E0 if l == 0 else E
                self.nb = JOBS0 if l == 0 else JOBS1
                self.per = self.nb * NGROUP
                hid = HID0 if l == 0 else HID1
                self.width = lambda hb: min(128, hid - 128 * hb)
                self.parts = {"in": hid, "out": self.nb * 128}
                if l:
                    self.parts = {"in": hid, "up": hid, "out": self.nb * 128}
                b_ = lambda name, shape, dt=F32: sb(name + n, shape, dt, stack)
                self.raw = {w: b_("raw_" + w, [128, c]) for w, c in self.parts.items()}
                self.hi = [{w: b_(f"hi{i}_" + w, [128, c], F32R) for w, c in self.parts.items()} for i in range(2)]
                self.lo = [{w: b_(f"lo{i}_" + w, [128, c], F32R) for w, c in self.parts.items()} for i in range(2)]
                self.gate = [b_(f"gate{i}_", [128, TOK]) for i in range(2)]
                self.h = [b_(f"h{i}_", [128, GROUP]) for i in range(RING)]
                self.h_hi = [b_(f"hh{i}_", [128, GROUP], F32R) for i in range(RING)]
                self.h_lo = [b_(f"hl{i}_", [128, GROUP], F32R) for i in range(RING)]
                self.act = [b_(f"act{i}_", [128, GROUP]) for i in range(RING)] if l else None
                self.b1 = [b_(f"b1_{i}_", [128, JOBS0]) for i in range(2)]
                self.bias_in = [s("bias_in_a"), s("bias_in_b")]
                self.weighted = b_("weighted", [128, GROUP])
                self.w_in, self.split = s("w_in"), s("split")
                self.gate_in = [s("gate_in_a"), s("gate_in_b")]
                self.h_ps, self.acted, self.multiplied = s("h_ps"), s("acted"), s("multiplied")
                self.hi_done, self.lo_done, self.h_used = s("hi_done"), s("lo_done"), s("h_used")
                self.y_added, self.y_read, self.y_zero, self.raw_split = s("y_added"), s("y_read"), s("y_zero"), s("raw_split")

            def loop(self, eng, body):
                body(0, 2)
                with eng.Fori(1, self.n // 2) as p:
                    body(p, 2)
                if self.n % 2:
                    body(self.n // 2, 1)

        def ffn_sync(sp, X, srcs, l):
            def body(pair, n):
                e0 = 2 * pair
                for i in range(n):
                    e = e0 + i
                    until(sp, X.raw_split, len(X.parts) * e)
                    for w in X.parts:
                        sp.dma_start(X.raw[w][:, :], srcs[w][span(e * 128, 128), :]).then_inc(X.w_in, 16)
                    if l == 0:
                        until(sp, X.hi_done, X.per * (e - 1))
                        sp.dma_start(X.b1[i][:, :], srcs["bias"][span(e * 128, 128), :]).then_inc(X.bias_in[i], 16)
                    if isinstance(e, int) and e == E:
                        continue
                    until(sp, X.y_read, NGROUP * (e - 1))
                    row = c_dram[l, span(e, 1), :] if not isinstance(e, int) else c_dram[l, e:e + 1, :]
                    sp.dma_start(X.gate[i][:, :], row.to_broadcast([128, TOK])).then_inc(X.gate_in[i], 16)
            X.loop(sp, body)

        def ffn_pool(p, X):
            p.memset(y[:, :], 0.0).then_inc(X.y_zero, 1)
            p.wait_ge(pool_own, 1)

            def body(pair, n):
                e0 = 2 * pair
                for i in range(n):
                    e = e0 + i
                    p.wait_ge(X.w_in, 16 * len(X.parts) * (e + 1))
                    until(p, X.h_used, X.per * (e - 1))
                    for k, w in enumerate(X.parts):
                        p.tensor_tensor(X.hi[i][w][:, :], X.raw[w][:, :], zeros[:, 0:X.parts[w]],
                                        ALU.add).then_inc(X.split, 1)
                        p.wait_ge(X.split, len(X.parts) * e + k + 1)
                        p.tensor_tensor(X.lo[i][w][:, :], X.raw[w][:, :], X.hi[i][w][:, :].bitcast(F32),
                                        ALU.subtract).then_inc(X.raw_split, 1)
            X.loop(p, body)

        def ffn_tensor(pe, X):
            def hidden(e, i, j, base):
                tg, hb = divmod(j % X.per, X.nb)
                width = X.width(hb)
                m = slice(tg * GROUP, (tg + 1) * GROUP)
                c = slice(hb * 128, hb * 128 + width)
                if j % X.per == 0:
                    pe.wait_ge(X.raw_split, len(X.parts) * (e + 1))
                if X.l == 0:
                    until(pe, X.hi_done, base + j - 3)
                    three(pe, bank[j % 4][0:width, :], X.hi[i]["in"][:, c], X.lo[i]["in"][:, c],
                          xt_hi[:, m], xt_lo[:, m]).then_inc(X.h_ps, 1)
                else:
                    until(pe, X.multiplied, base + j - 1)
                    for k, w in enumerate(("in", "up")):
                        ins = three(pe, bank[2 * (j % 2) + k][0:width, :], X.hi[i][w][:, c], X.lo[i][w][:, c],
                                    xt_hi[:, m], xt_lo[:, m])
                    ins.then_inc(X.h_ps, 1)

            def outward(j, base, ubase):
                i = (j // X.per) % 2
                tg, hb = divmod(j % X.per, X.nb)
                width = X.width(hb)
                unit = j // X.nb
                ps = bank[4 + unit % 2]
                if hb == 0:
                    until(pe, X.y_read, ubase + unit - 1)
                pe.wait_ge(X.hi_done, base + j + 1)
                pe.wait_ge(X.lo_done, base + j + 1)
                wc = slice(hb * 128, (hb + 1) * 128)
                hi, lo = X.hi[i]["out"][0:width, wc], X.lo[i]["out"][0:width, wc]
                hh, hl = X.h_hi[j % RING][0:width, :], X.h_lo[j % RING][0:width, :]
                pe.matmul(ps[:, :], lo, hh, start=(hb == 0), stop=False)
                pe.matmul(ps[:, :], hi, hl, start=False, stop=False)
                pe.matmul(ps[:, :], hi, hh, start=False, stop=(hb == X.nb - 1)).then_inc(X.h_used, 1)

            def body(pair, n):
                e0 = 2 * pair
                base, ubase = X.per * e0, NGROUP * e0
                for j in range(n * X.per):
                    hidden(e0 + j // X.per, j // X.per, j, base)
                    if not (isinstance(e0, int) and e0 == 0 and j < LAG):
                        outward(j - LAG, base, ubase)
            X.loop(pe, body)
            total_jobs = X.per * X.n
            tail = X.n - 1 if X.n % 2 else X.n - 2
            for j in range(total_jobs - LAG, total_jobs):
                outward(j - X.per * tail, X.per * tail, NGROUP * tail)
            for t in range(B):
                if t % 4 == 0:
                    if t == 0:
                        pe.wait_ge(X.y_read, NGROUP * X.n)
                        pe.wait_ge(X.y_added, NGROUP * E)
                    elif t >= 8:
                        pe.wait_ge(x_added, NGROUP * X.l + t // 4 - 1)
                ins = pe.transpose(bank[6 + (t // 4) % 2][:, (t % 4) * 128:(t % 4 + 1) * 128],
                                   y[:, t * S:(t + 1) * S], ident[:, :])
                if t % 4 == 3:
                    ins.then_inc(y_turned, 1)

        def ffn_scalar(act, X):
            def body(pair, n):
                e0 = 2 * pair
                base = X.per * e0
                for j in range(n * X.per):
                    e, hb = e0 + j // X.per, j % X.nb
                    width = X.width(hb)
                    r = j % RING
                    act.wait_ge(X.h_ps, base + j + 1)
                    if X.l == 0:
                        bias = X.b1[j // X.per][:, hb:hb + 1]
                        if j % X.per == 0:
                            act.wait_ge(X.bias_in[j // X.per], pair * 16 + 16)
                        until(act, X.lo_done, base + j - 3)
                        act.activation(X.h[r][:, :], bank[r][:, :], ACT.Gelu, bias=bias).then_inc(X.acted, 1)
                        until(act, X.h_used, base + j - 3)
                        act.activation(X.h_hi[r][:, :], bank[r][:, :], ACT.Gelu, bias=bias).then_inc(X.hi_done, 1)
                        continue
                    until(act, X.multiplied, base + j - 3)
                    act.activation(X.act[r][0:width, :], bank[2 * (j % 2)][0:width, :], ACT.Silu).then_inc(X.acted, 1)
                    if not (isinstance(e0, int) and e0 == 0 and j == 0):
                        high(base, j - 1)
            def high(base, j):
                width, r = X.width(j % X.nb), j % RING
                act.wait_ge(X.multiplied, base + j + 1)
                until(act, X.h_used, base + j - 3)
                act.activation(X.h_hi[r][0:width, :], X.h[r][0:width, :], ACT.Copy).then_inc(X.hi_done, 1)
            X.loop(act, body)
            if X.l:
                high(0, X.per * X.n - 1)

        def ffn_vector(v, X):
            v.wait_ge(X.y_zero, 1)

            def low(base, j):
                width, r = X.width(j % X.nb), j % RING
                v.wait_ge(X.hi_done, base + j + 1)
                until(v, X.h_used, base + j - 3)
                v.tensor_tensor(X.h_lo[r][0:width, :], X.h[r][0:width, :], X.h_hi[r][0:width, :].bitcast(F32),
                                ALU.subtract).then_inc(X.lo_done, 1)

            def gather(p, j):
                e0, base, ubase = 2 * p, 2 * X.per * p, 2 * NGROUP * p
                unit = j // X.nb
                tg = unit % NGROUP
                i = (unit // NGROUP) % 2
                e = e0 + unit // NGROUP
                m = slice(tg * GROUP, (tg + 1) * GROUP)
                v.wait_ge(X.h_used, base + j + 1)
                ps = bank[4 + unit % 2]
                if isinstance(e, int) and e == E:
                    v.wait_ge(X.y_added, NGROUP * E)
                    v.scalar_tensor_tensor(out=y[:, m], in0=ps[:, :], scalar=b2[:, E:E + 1], in1=y[:, m],
                                           op0=ALU.add, op1=ALU.add).then_inc(X.y_read, 1)
                    return
                if tg == 0:
                    v.wait_ge(X.gate_in[i], 16 * p + 16)
                gate = X.gate[i][:, m]
                until(v, X.y_added, ubase + unit)
                if X.l == 0:
                    v.scalar_tensor_tensor(out=X.weighted[:, :], in0=ps[:, :], scalar=b2[:, span(e, 1)], in1=gate,
                                           op0=ALU.add, op1=ALU.mult).then_inc(X.y_read, 1)
                else:
                    v.tensor_tensor(X.weighted[:, :], ps[:, :], gate, ALU.mult).then_inc(X.y_read, 1)
                v.wait_ge(X.y_read, ubase + unit + 1)
                v.tensor_tensor(y[:, m], y[:, m], X.weighted[:, :], ALU.add).then_inc(X.y_added, 1)

            def body(p, n):
                base = 2 * X.per * p
                zero = isinstance(p, int) and p == 0
                for j in range(n * X.per):
                    if X.l == 0:
                        low(base, j)
                    else:
                        width, r = X.width(j % X.nb), j % RING
                        v.wait_ge(X.acted, base + j + 1)
                        until(v, X.hi_done, base + j - 3)
                        v.tensor_tensor(X.h[r][0:width, :], bank[2 * (j % 2) + 1][0:width, :], X.act[r][0:width, :],
                                        ALU.mult).then_inc(X.multiplied, 1)
                        if not (zero and j == 0):
                            low(base, j - 1)
                    done = j - LAG - 1
                    if (done + 1) % X.nb == 0 and not (zero and done < 0):
                        gather(p, done)
            X.loop(v, body)
            tail = X.n - 1 if X.n % 2 else X.n - 2
            rest = X.per * (X.n - tail)
            if X.l:
                low(X.per * tail, rest - 1)
            for done in range(rest - LAG - 1, rest):
                if (done + 1) % X.nb == 0:
                    gather(tail // 2, done)
            for g in range(NGROUP):
                v.wait_ge(y_turned, NGROUP * X.l + g + 1)
                m = slice(g * GROUP, (g + 1) * GROUP)
                v.tensor_tensor(x[:, m], bank[6 + g % 2][:, :], x[:, m], ALU.add).then_inc(x_added, 1)
            v.wait_ge(x_added, NGROUP * (X.l + 1))
            v.sem_inc(phase, 1)

        y_turned, x_added, finished = sem("y_turned"), sem("x_added"), sem("finished")
        pool_own = sem("pool_own")
        bo_ready = sem("bo_ready")
        pool_n = [1]
        stacks = [ctx.enter_context(ExitStack()) for _ in range(4)]
        parts = []
        for l in range(2):
            with ExitStack() as st:
                A = Attention(l, st)
            with ExitStack() as st:
                X = Experts(l, st)
            parts.append((A, X))

        def att_loads(l, A):
            if l == 0:
                return [(A.raw["q"][:, :], a["wq0"]), (A.raw["k"][:, :], a["wk0"]), (A.wv[:, :], a["wv0"]),
                        (A.wo[:, :], a["wo0"]), (A.bq[:, :], a["bq"]), (A.bk[:, :], a["bk"]),
                        (A.bv[:, :], a["bv"].to_broadcast([128, D]))]
            return [(A.raw["q"][:, :], a["wq1"]), (A.raw["k"][:, :], a["wk1"]), (A.raw["v"][:, :], a["wv1"]),
                    (A.wo[:, :], a["wo1"])]

        first_loads = [(masks, "masks"), (ident, "ident"), (minus_half, "minus_half"), (expert_no, "expert_no"),
                       (gw[0], "gw0"), (gw[1], "gw1"), (b2, "b2"), (ct, "ct")]
        for l in range(2):
            parts[l][0].n_loads = len(att_loads(l, parts[l][0]))
        N_FIRST = len(first_loads) + 4

        block = ctx.enter_context(nc.Block())

        @block.sync
        def _(sp):
            sp.dma_start(x[:, :].rearrange("s (b d) -> s b d", b=B), a["x"].rearrange("b s d -> s b d")).then_inc(loaded, 16)
            for dst, name in first_loads:
                sp.dma_start(dst[:, :], a[name]).then_inc(loaded, 16)
            sp.dma_start(gb[:, :], a["gb"].to_broadcast([128, E])).then_inc(loaded, 16)
            for l in range(2):
                sp.dma_start(bo[l][:, :], a[f"bo{l}"].to_broadcast([128, D])).then_inc(loaded, 16)
            for l, (A, X) in enumerate(parts):
                if l:
                    sp.wait_ge(phase, 2)
                for dst, src in att_loads(l, A):
                    sp.dma_start(dst, src).then_inc(A.w_loaded, 16)
                sp.wait_ge(phase, 2 * l + 1)
                route_sync(sp, l)
                ffn_sync(sp, X, {"in": a["w1_0"], "out": a["w2_0"], "bias": a["b1"]} if l == 0 else
                         {"in": a["w1_1"], "up": a["w2_1"], "out": a["w3_1"]}, l)
            sp.wait_ge(phase, 4)
            sp.dma_start(out.rearrange("b s d -> s b d"), x[:, :].rearrange("s (b d) -> s b d", b=B)).then_inc(finished, 16)
            sp.wait_ge(finished, 16)

        @block.tensor
        def _(pe):
            pe.wait_ge(loaded, 16 * N_FIRST)
            for l, (A, X) in enumerate(parts):
                norm_tensor(pe, 2 * l)
                if l == 0:
                    pe.wait_ge(ctx_split, 1)
                pe.wait_ge(xt_ready, NGROUP * (2 * l + 1))
                att_tensor(pe, A)
                pe.wait_ge(phase, 2 * l + 1)
                norm_tensor(pe, 2 * l + 1)
                route_tensor(pe, l)
                pe.wait_ge(xt_ready, NGROUP * (2 * l + 2))
                ffn_tensor(pe, X)
                pe.wait_ge(phase, 2 * l + 2)

        @block.scalar
        def _(act):
            act.wait_ge(loaded, 16 * N_FIRST)
            for l, (A, X) in enumerate(parts):
                norm_scalar(act, 2 * l)
                act.wait_ge(phase, 2 * l) if l else None
                att_scalar(act, A)
                act.wait_ge(phase, 2 * l + 1)
                norm_scalar(act, 2 * l + 1)
                route_scalar(act, l)
                ffn_scalar(act, X)
                act.wait_ge(phase, 2 * l + 2)

        @block.gpsimd
        def _(p):
            p.memset(zeros[:, :], 0.0).then_inc(pool_own, 1)
            p.wait_ge(loaded, 16 * N_FIRST)
            for l, (A, X) in enumerate(parts):
                norm_pool(p, 2 * l)
                p.wait_ge(xn_ready, B * (2 * l + 1))
                xv = x[:, :].rearrange("p (b d) -> p b d", b=B)
                bb = bo[l][:, :].rearrange("p (o d) -> p o d", o=1).to_broadcast([128, B, D])
                p.tensor_tensor(xv, xv, bb, ALU.add).then_inc(bo_ready, 1)
                att_pool(p, A)
                p.wait_ge(phase, 2 * l + 1)
                norm_pool(p, 2 * l + 1)
                ffn_pool(p, X)
                p.wait_ge(phase, 2 * l + 2)

        @block.vector
        def _(v):
            v.wait_ge(loaded, 16 * N_FIRST)
            k = seq(v.tensor_copy(ct_hi[:, :], ct[:, :]))
            v.wait_ge(dve, k)
            v.tensor_tensor(ct_lo[:, :], ct[:, :], ct_hi[:, :].bitcast(F32), ALU.subtract).then_inc(ctx_split, 1)
            for l, (A, X) in enumerate(parts):
                norm_vector(v, 2 * l)
                v.wait_ge(bo_ready, l + 1)
                att_vector(v, A)
                norm_vector(v, 2 * l + 1)
                route_vector(v, l)
                ffn_vector(v, X)


def kernel(**inputs):
    import concourse.bacc as bacc
    from concourse.bass_utils import run_bass_kernel_spmd

    f = {n: np.asarray(v) for n, v in inputs.items()}
    rows = np.arange(128)
    copy_no, head_no = rows // 32, (rows % 32) // HD0
    masks = np.stack([copy_no >= 2, copy_no % 2 == 1] + [head_no == j for j in range(4)], axis=1)

    def replicated(w):
        wt = w.T.reshape(D, QUADS, 1, 32)
        return np.broadcast_to(wt, (D, QUADS, 4, 32)).reshape(D, QUADS * 128)

    def replicated_bias(b):
        bt = b.reshape(QUADS, 1, 32)
        return np.broadcast_to(bt, (QUADS, 4, 32)).reshape(QUADS, 128).T

    def chunks(w, width):
        e, hid, o = w.shape
        whole = np.zeros((e, width, o), w.dtype)
        whole[:, :hid] = w
        return whole.reshape(e, width // 128, 128, o).transpose(0, 2, 1, 3).reshape(e * 128, -1)

    wo0 = np.zeros((QUADS, 4, 32, D), f["L0_xattn_Wo"].dtype)
    wo0[:, :, :HD0] = f["L0_xattn_Wo"].T.reshape(QUADS, 4, HD0, D)
    arrays = {
        "x": f["x"],
        "ct": f["ctx_1024"].reshape(TOK, D).T,
        "masks": masks.astype(np.float32),
        "ident": np.eye(128, dtype=np.float32),
        "minus_half": np.full((128, B), -0.5, np.float32),
        "expert_no": np.broadcast_to(np.repeat(np.arange(E, dtype=np.float32), B), (128, E * B)),
        "wq0": replicated(f["L0_xattn_Wq"]), "wk0": replicated(f["L0_xattn_Wk"]),
        "wv0": f["L0_xattn_Wv"].T,
        "wo0": wo0.reshape(QUADS, 128, D).transpose(1, 0, 2).reshape(128, QUADS * D),
        "bq": replicated_bias(f["L0_xattn_bq"]), "bk": replicated_bias(f["L0_xattn_bk"]),
        "bv": f["L0_xattn_bv"].reshape(1, D),
        "bo0": f["L0_xattn_bo"].reshape(1, D), "bo1": f["L1_xattn_bo"].reshape(1, D),
        "gw0": f["L0_ffn_gate_w"], "gb": f["L0_ffn_gate_b"].reshape(1, E),
        "w1_0": np.concatenate([f["L0_ffn_w1"], f["L0_ffn_ws1"][None]]).reshape(E0 * 128, HID0),
        "w2_0": chunks(np.concatenate([f["L0_ffn_w2"], f["L0_ffn_ws2"][None]]), HID0),
        "b1": np.concatenate([f["L0_ffn_b1"], f["L0_ffn_bs1"][None]]).reshape(E0, JOBS0, 128).transpose(0, 2, 1).reshape(E0 * 128, JOBS0),
        "b2": np.concatenate([f["L0_ffn_b2"], f["L0_ffn_bs2"][None]]).T,
        "wq1": f["L1_xattn_Wq"], "wk1": f["L1_xattn_Wk"], "wv1": f["L1_xattn_Wv"],
        "wo1": f["L1_xattn_Wo"].reshape(8, 128, D).transpose(1, 0, 2).reshape(128, 8 * D),
        "gw1": f["L1_ffn_Wg"].T,
        "w1_1": f["L1_ffn_W1"].transpose(0, 2, 1).reshape(E * 128, HID1),
        "w2_1": f["L1_ffn_W2"].transpose(0, 2, 1).reshape(E * 128, HID1),
        "w3_1": chunks(f["L1_ffn_W3"].transpose(0, 2, 1), JOBS1 * 128),
    }
    nc = bacc.Bacc("TRN2", target_bir_lowering=False, num_devices=1)
    named, aps = {}, {}
    for name, value in arrays.items():
        value = np.ascontiguousarray(value)
        named["in_" + name] = value
        aps[name] = nc.dram_tensor("in_" + name, value.shape, mybir.dt.from_np(value.dtype), kind="ExternalInput").ap()
    result = nc.dram_tensor("result", (B, S, D), F32, kind="ExternalOutput").ap()
    build(nc, aps, result)
    r = run_bass_kernel_spmd(nc, [named], core_ids=[0])
    return r.results[0]["result"]
```

```python
from contextlib import ExitStack

import numpy as np

import concourse.bass as bass
from concourse import mybir

F32 = mybir.dt.float32
F32R = mybir.dt.float32r
U32 = mybir.dt.uint32
ALU = mybir.AluOpType
ACT = mybir.ActivationFunctionType
AX_X = mybir.AxisListType.X

B, S, D = 16, 128, 128
TOK = B * S
H = 16
HD0, HD1 = 8, 64
INNER1 = H * HD1
E = 8
HID0, HID1 = 512, 352
E0 = E + 1
EPS = 1e-5

GROUP = 512
NG = TOK // GROUP
BPG = GROUP // S
QUADS = H // 4
UNITS = QUADS * BPG
NU = NG * UNITS
AHEAD = 4
SLOTS = 6
SCALE0 = 1.0 / (D / H) ** 0.5
SCALE1 = HD1 ** -0.5
JOBS0 = HID0 // 128
JOBS1 = -(-HID1 // 128)
WCOLS0 = HID0 + JOBS0 * 128
WCOLS1 = 2 * HID1 + JOBS1 * 128
WCOLS = max(WCOLS0, WCOLS1)
WCHUNK = WCOLS // 2
RING = 4
LAG = 3


def span(start, size):
    return slice(start, start + size) if isinstance(start, int) else bass.ds(start, size)


def until(eng, sem, value):
    if not isinstance(value, int) or value > 0:
        eng.wait_ge(sem, value)


def group(g):
    return slice(g * GROUP, (g + 1) * GROUP)


def tile(t):
    return slice(t * 128, (t + 1) * 128)


NORMS = [(2 * l + p, g) for l in range(2)
         for p, g in ((0, 0), (0, 1), (0, 2), (1, 0), (0, 3), (1, 1), (1, 2), (1, 3))]
NORM_NO = {item: n for n, item in enumerate(NORMS)}
SPLIT_NO = {item: n for n, item in enumerate(item for item in NORMS if item[0])}
CONTEXT_STEPS = [13, 28, 45, 51]
OWN_STEPS = [{"stats": 1, "power": 2, "scale": 3, "turn": 4, "copy": 5, "bias": 6},
             {"y_turn": 0, "y_add": 1, "stats": 4, "power": 5, "scale": 6, "turn": 7, "copy": 8, "bias": 8,
              "split": 9}]
NEXT_STEPS = [{"stats": 9, "power": 10, "scale": 11, "turn": 12, "copy": 13, "split": 15},
              {"stats": 6, "power": 7, "scale": 8, "turn": 9, "copy": 10, "split": 11}]


def norm_at(l, n, stage):
    g, u = divmod(n, UNITS)
    at = []
    if g < NG - 1 and OWN_STEPS[l].get(stage) == u:
        at.append((2 * l, g + 1))
    if 0 < g < NG and NEXT_STEPS[l].get(stage) == u:
        at.append((2 * l + 1, g - 1))
    return at


def side_jobs(layer):
    at = {-1: [("V", b) for b in range(0, BPG, 1 + layer)]}
    for n in range(NU):
        g, u = divmod(n, UNITS)
        at[n] = []
        if layer == 0:
            if u >= 14 and g < NG - 1:
                at[n].append(("V", BPG * (g + 1) + u - 14))
            if u <= 1 and g:
                at[n].append(("V", BPG * g + u + 2))
            batches = [u - 3] if 3 <= u < 3 + BPG else []
        else:
            if n % 2 == 0 and n + AHEAD < NU:
                at[n].append(("V", n + AHEAD))
            batches = {1: [0], 2: [1], 3: [2], 5: [3]}.get(u, [])
        if g:
            at[n] += [("O", BPG * (g - 1) + b) for b in batches]
    at[NU] = [("O", BPG * (NG - 1) + b) for b in range(BPG)]
    return at


ROUTES = [(0, 0, B)] + [(1, BPG * g, BPG) for g in range(NG)]


def route_at(l, n):
    g, u = divmod(n, UNITS)
    if l == 0:
        return None, ()
    if u == 0:
        return g - 1, ("rows_copy",) if g > 1 else ()
    return g, {11: ("logits",), 12: (0, 1, 2), 13: (3, 4, 5), 14: (6, 7), 15: ("rows_turn",)}.get(u, ()) if g else ()


class Turns:

    def __init__(self, psum, filled, read):
        self.psum, self.filled, self.read = psum, filled, read
        self.order = []

    def before(self, job):
        self.order.append(job)
        return len(self.order) - 1

    def upto(self, job):
        return self.order.index(job) + 1

    def done(self, job):
        return self.order.index(job) + 1


def build(nc, a, out):
    gate_rows = nc.dram_tensor("gate_rows", [2, E, TOK], F32, kind="Internal").ap()

    with ExitStack() as ctx:
        def sb(name, shape, dt=F32, stack=ctx):
            return stack.enter_context(nc.sbuf_tensor(name, shape, dt))

        def sem(name):
            return ctx.enter_context(nc.semaphore(name))

        bank = [ctx.enter_context(nc.psum_tensor(f"bank{i}", [128, GROUP], F32)) for i in range(8)]

        x = sb("x", [128, TOK])
        xn = sb("xn", [128, TOK])
        xt = sb("xt", [128, TOK])
        xt_hi, xt_lo = sb("xt_hi", [128, TOK], F32R), sb("xt_lo", [128, TOK], F32R)
        ct = sb("ct", [128, TOK])
        ct_hi, ct_lo = sb("ct_hi", [128, TOK], F32R), sb("ct_lo", [128, TOK], F32R)
        y = sb("y", [128, TOK])
        ident = sb("ident", [128, 128])
        zeros = sb("zeros", [128, WCHUNK])
        masks = sb("masks", [128, H])
        stats, meanvar = sb("stats", [128, B * 6]), sb("meanvar", [128, B * 2])
        veps, minus_half, rstd = sb("veps", [128, B]), sb("minus_half", [128, B]), sb("rstd", [128, B])
        euler = sb("euler", [128, B])
        gw = [sb(f"gw{l}", [128, E]) for l in range(2)]
        gb = sb("gb", [128, E])
        expert_no = sb("expert_no", [128, E * B])
        logit, top, topi = sb("logit", [128, B * E]), sb("top", [128, B * 8]), sb("topi", [128, B * 8], U32)
        topf, gweight = sb("topf", [128, B * 2]), sb("gweight", [128, B * 2])
        gdiff, gexp, gone = sb("gdiff", [128, B]), sb("gexp", [128, B]), sb("gone", [128, B])
        hot = [sb(f"hot{i}", [128, E * B]) for i in range(2)]
        combine, combine_t = sb("combine", [128, E * B]), sb("combine_t", [128, 128])
        b2 = sb("b2", [128, E0])
        bo = [sb(f"bo{l}", [128, D]) for l in range(2)]
        b1 = [sb(f"b1_{i}", [128, JOBS0]) for i in range(2)]
        negmax, total, rtotal = [sb(n, [128, SLOTS * 4]) for n in ("negmax", "total", "rtotal")]
        w_raw = sb("w_raw", [128, WCOLS])
        w_hi = [sb(f"w_hi{i}", [128, WCOLS], F32R) for i in range(2)]
        w_lo = [sb(f"w_lo{i}", [128, WCOLS], F32R) for i in range(2)]
        wkq_hi, wkq_lo = sb("wkq_hi", [128, H * D], F32R), sb("wkq_lo", [128, H * D], F32R)
        wv_hi, wv_lo = sb("wv_hi", [128, INNER1], F32R), sb("wv_lo", [128, INNER1], F32R)
        wo1 = sb("wo1", [128, 8 * D])

        x_in, ct_in = [sem(f"x_in{g}") for g in range(NG)], [sem(f"ct_in{g}") for g in range(NG)]
        const_in, late_in, wo1_in = sem("const_in"), sem("late_in"), sem("wo1_in")
        dve, pool_own = sem("dve"), sem("pool_own")
        ct_split = sem("ct_split")
        norm_in, pow_done, xn_ready = sem("norm_in"), sem("pow_done"), sem("xn_ready")
        xt_ready = sem("xt_ready")
        bank2, bank3, bank6, bank7 = [Turns(bank[i], sem(f"bank{i}_filled"), sem(f"bank{i}_read")) for i in (2, 3, 6, 7)]
        bo_added, bias_scaled = sem("bo_added"), sem("bias_scaled")
        aw_in, aw_split = sem("aw_in"), sem("aw_split")
        route_diff, route_exp = sem("route_diff"), sem("route_exp")
        combined = sem("combined")
        stored, finished = sem("stored"), sem("finished")

        dve_n = [0]

        def seq(ins):
            dve_n[0] += 1
            ins.then_inc(dve, 1)
            return dve_n[0]

        def norm_stats(v, phase, g):
            tiles = range(g * BPG, (g + 1) * BPG)
            if phase == 0:
                v.wait_ge(x_in[g], 16)
            elif phase == 2:
                v.wait_ge(bank7.read, bank7.done(("y", 0, g)))
            else:
                last = ("O", phase // 2, (g + 1) * BPG - 1)
                turns = layers[phase // 2][0].side_turns(*last[::2])
                v.wait_ge(turns.read, turns.done(last))
            for t in tiles:
                k = seq(v.bn_stats(stats[:, t * 6:t * 6 + 6], x[:, tile(t)]))
            v.wait_ge(dve, k)
            for t in tiles:
                k = seq(v.bn_aggr(meanvar[:, 2 * t:2 * t + 2], stats[:, t * 6:t * 6 + 6]))
            v.wait_ge(dve, k)
            var = meanvar[:, 2 * tiles[0]:2 * tiles[0] + 2 * BPG].rearrange("p (t k) -> p t k", k=2)[:, :, 1]
            v.tensor_scalar(veps[:, tiles[0]:tiles[0] + BPG], var, EPS, None, ALU.add).then_inc(norm_in, 1)

        def norm_power(p, phase, g):
            p.wait_ge(norm_in, NORM_NO[phase, g] + 1)
            t = g * BPG
            p.tensor_tensor(rstd[:, t:t + BPG], veps[:, t:t + BPG], minus_half[:, 0:BPG], ALU.pow).then_inc(pow_done, 1)

        def norm_scale(v, phase, g):
            v.wait_ge(pow_done, NORM_NO[phase, g] + 1)
            for t in range(g * BPG, (g + 1) * BPG):
                ins = v.tensor_scalar(xn[:, tile(t)], x[:, tile(t)], meanvar[:, 2 * t:2 * t + 1],
                                      rstd[:, t:t + 1], ALU.subtract, ALU.mult)
            ins.then_inc(xn_ready, 1)

        def norm_turns(phase, g):
            return bank7 if (phase == 2 and g) or (phase == 3 and g < NG - 1) else bank6

        def norm_turn(pe, phase, g):
            turns = norm_turns(phase, g)
            until(pe, turns.read, turns.before(("norm", phase, g)))
            pe.wait_ge(xn_ready, NORM_NO[phase, g] + 1)
            for b in range(BPG):
                ins = pe.transpose(turns.psum[:, tile(b)], xn[:, tile(g * BPG + b)], ident[:, :])
            ins.then_inc(turns.filled, 1)

        def norm_copy(act, phase, g):
            turns = norm_turns(phase, g)
            act.wait_ge(turns.filled, turns.upto(("norm", phase, g)))
            act.activation(xt[:, group(g)], turns.psum[:, :], ACT.Copy).then_inc(turns.read, 1)

        def norm_split(v, phase, g):
            turns = norm_turns(phase, g)
            v.wait_ge(turns.read, turns.done(("norm", phase, g)))
            k = seq(v.tensor_copy(xt_hi[:, group(g)], xt[:, group(g)]))
            v.wait_ge(dve, k)
            v.tensor_tensor(xt_lo[:, group(g)], xt[:, group(g)], xt_hi[:, group(g)].bitcast(F32),
                            ALU.subtract).then_inc(xt_ready, 1)

        def split_context(v, g):
            v.wait_ge(ct_in[g], 16)
            k = seq(v.tensor_copy(ct_hi[:, group(g)], ct[:, group(g)]))
            v.wait_ge(dve, k)
            v.tensor_tensor(ct_lo[:, group(g)], ct[:, group(g)], ct_hi[:, group(g)].bitcast(F32),
                            ALU.subtract).then_inc(ct_split, 1)

        def add_bias(p, phase, g):
            p.wait_ge(xn_ready, NORM_NO[phase, g] + 1)
            xv = x[:, group(g)].rearrange("p (b d) -> p b d", b=BPG)
            bb = bo[phase // 2][:, :].rearrange("p (o d) -> p o d", o=1).to_broadcast([128, BPG, D])
            p.tensor_tensor(xv, xv, bb, ALU.add).then_inc(bo_added, 1)

        def y_turn(pe, l, g):
            X = layers[l][1]
            pe.wait_ge(X.y_added, NG * (X.n - 2) + g + 1)
            until(pe, bank7.read, bank7.before(("y", l, g)))
            for b in range(BPG):
                ins = pe.transpose(bank[7][:, tile(b)], y[:, tile(g * BPG + b)], ident[:, :])
            ins.then_inc(bank7.filled, 1)

        def y_add(v, l, g):
            v.wait_ge(bank7.filled, bank7.upto(("y", l, g)))
            v.tensor_tensor(x[:, group(g)], bank[7][:, :], x[:, group(g)], ALU.add).then_inc(bank7.read, 1)

        def logits_tensor(pe, r):
            l, t0, nt = ROUTES[r]
            last = 2 * l + 1, (t0 + nt) // BPG - 1
            turns = norm_turns(*last)
            pe.wait_ge(turns.read, turns.done(("norm",) + last))
            until(pe, bank7.read, bank7.before(("logits", r)))
            for i in range(nt):
                ins = pe.matmul(bank[7][:, i * E:(i + 1) * E], xt[:, tile(t0 + i)], gw[l][:, :], start=True, stop=True)
            ins.then_inc(bank7.filled, 1)

        def rows_tensor(pe, r):
            l, t0, nt = ROUTES[r]
            pe.wait_ge(combined, r + 1)
            until(pe, bank7.read, bank7.before(("rows", r)))
            pe.transpose(bank[7][0:E * nt, 0:128], combine[:, 0:E * nt], ident[:, :]).then_inc(bank7.filled, 1)

        route_k = {}

        def route_vector(v, r, step):
            l, t0, nt = ROUTES[r]
            lg = logit[:, 0:nt * E].rearrange("p (t e) -> p t e", e=E)
            tops = top[:, 0:nt * 8].rearrange("p (t k) -> p t k", k=8)
            two = lambda buf: buf[:, 0:2 * nt].rearrange("p (t k) -> p t k", k=2)
            w = two(gweight)
            numbers = expert_no[:, :].rearrange("p (e t) -> p e t", t=B)[:, :, 0:nt]
            by_expert = lambda buf: buf[:, 0:E * nt].rearrange("p (e t) -> p e t", t=nt)
            column = lambda buf, i: two(buf)[:, :, i].rearrange("p (o t) -> p o t", o=1).to_broadcast([128, E, nt])
            if step == 1:
                v.wait_ge(bank7.read, bank7.done(("logits", r)))
            elif step:
                v.wait_ge(dve, route_k[0])
            if step == 0:
                v.wait_ge(bank7.filled, bank7.upto(("logits", r)))
                ps = bank[7][:, 0:nt * E].rearrange("p (t e) -> p t e", e=E)
                if l == 0:
                    bias = gb[:, :].rearrange("p (o e) -> p o e", o=1).to_broadcast([128, nt, E])
                    v.tensor_tensor(lg, ps, bias, ALU.add).then_inc(bank7.read, 1)
                else:
                    v.tensor_copy(lg, ps).then_inc(bank7.read, 1)
                return
            elif step == 1:
                for i in range(nt):
                    k = seq(v.max(top[:, i * 8:(i + 1) * 8], logit[:, i * E:(i + 1) * E]))
            elif step == 2:
                for i in range(nt):
                    k = seq(v.max_index(topi[:, i * 8:(i + 1) * 8], top[:, i * 8:(i + 1) * 8],
                                        logit[:, i * E:(i + 1) * E]))
            elif step == 3:
                k = seq(v.tensor_copy(two(topf), topi[:, 0:nt * 8].rearrange("p (t k) -> p t k", k=8)[:, :, 0:2]))
                if l:
                    k = seq(v.tensor_copy(w, tops[:, :, 0:2]))
                else:
                    v.tensor_tensor(gdiff[:, :], tops[:, :, 1], tops[:, :, 0], ALU.subtract).then_inc(route_diff, 1)
            elif step == 4:
                for i in range(2):
                    k = seq(v.tensor_tensor(by_expert(hot[i]), numbers, column(topf, i), ALU.is_equal))
                if l == 0:
                    v.wait_ge(route_exp, 1)
                    k = seq(v.tensor_scalar(gone[:, :], gexp[:, :], 1.0, None, ALU.add))
            elif step == 5:
                if l == 0:
                    k = seq(v.reciprocal(w[:, :, 0], gone[:, :]))
                    v.wait_ge(dve, k)
                    k = seq(v.tensor_tensor(w[:, :, 1], gexp[:, :], w[:, :, 0], ALU.mult))
                else:
                    k = route_k[0]
            elif step == 6:
                for i in range(2):
                    k = seq(v.tensor_tensor(by_expert(hot[i]), by_expert(hot[i]), column(gweight, i), ALU.mult))
            elif step == 7:
                v.tensor_tensor(combine[:, 0:E * nt], hot[0][:, 0:E * nt], hot[1][:, 0:E * nt],
                                ALU.add).then_inc(combined, 1)
                return
            route_k[0] = k

        def rows_vector(v, r):
            l, t0, nt = ROUTES[r]
            v.wait_ge(bank7.filled, bank7.upto(("rows", r)))
            until(v, stored, 16 * r)
            v.tensor_copy(combine_t[0:E * nt, :], bank[7][0:E * nt, 0:128]).then_inc(bank7.read, 1)

        def route_power(p):
            p.wait_ge(route_diff, 1)
            p.tensor_tensor(gexp[:, :], euler[:, :], gdiff[:, :], ALU.pow).then_inc(route_exp, 1)

        def route_sync(sp, r):
            l, t0, nt = ROUTES[r]
            sp.wait_ge(bank7.read, bank7.done(("rows", r)))
            rows = gate_rows[l].rearrange("e (t s) -> e t s", t=B)[:, t0:t0 + nt, :]
            src = combine_t[0:E * nt, :]
            sp.dma_start(rows if nt < B else rows.rearrange("e t s -> (e t) s"), src).then_inc(stored, 16)
            sp.wait_ge(stored, 16 * (r + 1))

        class Attention:

            def __init__(self, l, stack):
                self.l = l
                n = f"{l}"
                s = lambda name: sem(name + n)
                self.scored, self.maxed, self.exped = s("scored"), s("maxed"), s("exped")
                self.inverted, self.normed = s("inverted"), s("normed")
                self.turned, self.turned_a, self.turned_v = s("turned"), s("turned_a"), s("turned_v")
                self.weighed, self.out_copied = s("weighed"), s("out_copied")
                b_ = lambda name, shape, dt=F32: sb(name + n, shape, dt, stack)
                self.p = [b_(f"p{i}_", [128, 512]) for i in range(SLOTS)]
                self.pt = [b_(f"pt{i}_", [128, 512]) for i in range(2)]
                if l == 0:
                    self.w_loaded, self.cleared = s("w_loaded"), s("cleared")
                    self.keys_v, self.keys_p = s("keys_v"), s("keys_p")
                    self.k = [b_(f"k{i}_", [128, BPG * 4 * S]) for i in range(2)]
                    self.w = {w: b_("w" + w, [128, D]) for w in "kqv"}
                    self.wo = b_("wo", [128, QUADS * D])
                    self.bias = {w: b_("b" + w, [128, 1]) for w in "qk"}
                    self.bq_scaled, self.bv = b_("bq_scaled", [128, 1]), b_("bv", [128, D])
                    self.q = [b_(f"q{i}_", [128, GROUP]) for i in range(2)]
                    self.all_k = [b_(f"all_k{i}_", [128, GROUP]) for i in range(2)]
                    self.v = b_("v", [128, BPG * H * 32])
                    self.ot = b_("ot", [128, (QUADS + 1) * GROUP])
                else:
                    self.keys_high = s("keys_high")
                    self.wo = wo1
                    self.k_hi, self.k_lo = [None] * 2, [None] * 2
                    for i in (1, 0):
                        if i == 0:
                            self.v = [b_(f"v{i}_", [128, BPG * 256]) for i in range(2)]
                            self.ot = b_("ot", [128, 8 * GROUP])
                        self.k_hi[i] = b_(f"k_hi{i}_", [128, BPG * 4 * S], F32R)
                        self.k_lo[i] = b_(f"k_lo{i}_", [128, BPG * 4 * S], F32R)
                self.qk_jobs = 2 if l == 0 else 4
                self.side_at = side_jobs(l)
                self.out_per = 4 if l == 0 else 2

            def early_sides(self, n):
                early = self.l == 0 or n % UNITS == 0 or len(self.side_at[n]) > 1
                return [job for job in self.side_at[n] if job[0] == "V" and early]

            def late_sides(self, n):
                return [job for job in self.side_at[n] if job not in self.early_sides(n)]

            def qk_turns(self, block, job):
                return bank3 if self.l <= block < 2 and job % 2 else bank6

            def copied(self, n):
                if self.l:
                    return self.turned_a, n + 1
                return (self.turned_v if n % 2 else self.turned_a), n // 2 + 1

            def ot_slot(self, g, c):
                return c if self.l else (QUADS * g + c) % (QUADS + 1)

            def side_turns(self, name, item):
                spare = name == "V" and item < BPG or name == "O" and item >= BPG * (NG - 1)
                return bank2 if spare and (item // 2 if self.l and name == "V" else item) % 2 else bank7

            def qk_at(self, n):
                if self.l == 0:
                    g, u = divmod(n, UNITS)
                    return [(QUADS * (g + 1), (u - 5) // 2)] if u in (5, 7) and g < NG - 1 else []
                block, job = divmod(n + 9, 4)
                return [(block, job)] if 2 <= block < QUADS * NG else []

        def three(pe, ps, w_hi, w_lo, m_hi, m_lo):
            pe.matmul(ps, w_lo, m_hi, start=True, stop=False)
            pe.matmul(ps, w_hi, m_lo, start=False, stop=False)
            return pe.matmul(ps, w_hi, m_hi, start=False, stop=True)

        def keys_tensor(pe, A, block, job):
            g, quad = divmod(block, QUADS)
            turns, at = A.qk_turns(block, job), tile(4 * quad + job)
            until(pe, turns.read, turns.before(("qk", 1, block, job)))
            pe.wait_ge(ct_split, g + 1)
            three(pe, turns.psum[:, :], wkq_hi[:, at], wkq_lo[:, at],
                  ct_hi[:, group(g)], ct_lo[:, group(g)]).then_inc(turns.filled, 1)

        def by_batch(buf, job):
            return buf[:, :].rearrange("p (b h s) -> p b h s", b=BPG, h=4)[:, :, job, :]

        def keys_high(act, A, block, job):
            turns = A.qk_turns(block, job)
            act.wait_ge(turns.filled, turns.upto(("qk", 1, block, job)))
            until(act, A.scored, BPG * (block - 1))
            act.activation(by_batch(A.k_hi[block % 2], job), turns.psum[:, :].rearrange("p (b s) -> p b s", b=BPG),
                           ACT.Copy).then_inc(A.keys_high, 1)

        def keys_low(v, A, block, job):
            turns = A.qk_turns(block, job)
            v.wait_ge(A.keys_high, 4 * block + job + 1)
            v.tensor_tensor(by_batch(A.k_lo[block % 2], job), turns.psum[:, :].rearrange("p (b s) -> p b s", b=BPG),
                            by_batch(A.k_hi[block % 2], job).bitcast(F32), ALU.subtract).then_inc(turns.read, 1)

        def att_tensor(pe, A):
            l = A.l

            def qk_job(block, job):
                if l:
                    keys_tensor(pe, A, block, job)
                    return
                g = block // QUADS
                turns, w = A.qk_turns(block, job), "kq"[job]
                until(pe, turns.read, turns.before(("qk", l, block, job)))
                if w == "k":
                    pe.wait_ge(ct_in[g], 16)
                else:
                    pe.wait_ge(bank6.read, bank6.done(("norm", 0, g)))
                pe.matmul(turns.psum[:, :], A.w[w][:, :], (xt if w == "q" else ct)[:, group(g)],
                          start=True, stop=True).then_inc(turns.filled, 1)

            def side_job(name, item):
                turns = A.side_turns(name, item)
                until(pe, turns.read, turns.before((name, l, item)))
                side_ps = turns.psum[:, 0:D if name == "O" or l == 0 else 512]
                if name == "V" and l == 0:
                    t = item
                    pe.wait_ge(ct_in[t // BPG], 16)
                    ins = pe.matmul(side_ps, ct[:, t * S:(t + 1) * S], A.w["v"][:, :], start=True, stop=True)
                elif name == "V":
                    g, u = divmod(item, UNITS)
                    quad, b = divmod(u, BPG)
                    w = slice(quad * 256, (quad + 1) * 256)
                    for k in range(2):
                        c = tile(g * BPG + b + k)
                        ins = three(pe, side_ps[:, k * 256:(k + 1) * 256], ct_hi[:, c], ct_lo[:, c], wv_hi[:, w], wv_lo[:, w])
                else:
                    g, b = divmod(item, BPG)
                    pe.wait_ge(A.out_copied, (g + 1) * UNITS // A.out_per - (1 if l and b < 2 else 0))
                    parts = QUADS if l == 0 else 8
                    for i in range(parts):
                        at = A.ot_slot(g, i) * GROUP
                        ins = pe.matmul(side_ps, A.ot[:, at + b * S:at + (b + 1) * S],
                                        A.wo[:, i * D:(i + 1) * D], start=(i == 0), stop=(i == parts - 1))
                ins.then_inc(turns.filled, 1)

            def score(n):
                block, b = divmod(n, BPG)
                g = block // QUADS
                ps = bank[n % 2]
                if l == 0:
                    queries = block - block % QUADS, 1
                    turns = A.qk_turns(*queries)
                    pe.wait_ge(turns.read, turns.done(("qk", 0) + queries))
                    pe.wait_ge(A.keys_v, block + 1)
                    pe.wait_ge(A.keys_p, block + 1)
                else:
                    turns = A.qk_turns(block, 3)
                    pe.wait_ge(turns.read, turns.done(("qk", l, block, 3)))
                    pe.wait_ge(xt_ready, SPLIT_NO[2, g] + 1)
                until(pe, A.exped, n - 1)
                keys = slice(b * 512, (b + 1) * 512)
                if l == 0:
                    ins = pe.matmul(ps[:, :], A.q[g % 2][:, tile(b)], A.k[block % 2][:, keys], start=True, stop=True)
                else:
                    t, k_hi, k_lo = tile(g * BPG + b), A.k_hi[block % 2], A.k_lo[block % 2]
                    ins = three(pe, ps[:, :], xt_hi[:, t], xt_lo[:, t], k_hi[:, keys], k_lo[:, keys])
                ins.then_inc(A.scored, 1)

            def turn(n):
                pe.wait_ge(A.normed, n + 1)
                if n < 2:
                    spare = (bank2, bank3)[n]
                    pe.wait_ge(spare.read, len(spare.order))
                else:
                    pe.wait_ge(*A.copied(n - 2))
                for j in range(4):
                    ins = pe.transpose(bank[2 + n % 2][:, j * 128:(j + 1) * 128],
                                       A.p[n % SLOTS][:, j * 128:(j + 1) * 128], ident[:, :])
                ins.then_inc(A.turned, 1)

            def weigh(n):
                block, b = divmod(n, BPG)
                quad = block % QUADS
                g = n // UNITS
                pe.wait_ge(*A.copied(n))
                chunk = n // A.out_per
                ps = bank[4 + chunk % 2]
                if n % A.out_per == 0:
                    until(pe, A.out_copied, chunk - 1)
                v_item = BPG * g + b if l == 0 else n - n % 2
                turns = A.side_turns("V", v_item)
                pe.wait_ge(turns.read, turns.done(("V", l, v_item)))
                pt = A.pt[n % 2]
                for j in range(4):
                    if l == 0:
                        at = (b * H + 4 * quad + j) * 32
                        ins = pe.matmul(ps[32 * j:32 * j + 32, b * 128:(b + 1) * 128], A.v[:, at:at + 32],
                                        pt[:, j * 128:(j + 1) * 128], start=True, stop=True)
                    else:
                        pair, half = divmod(j, 2)
                        at = b * 256 + j * 64
                        col = pair * 256 + (b % 2) * 128
                        ins = pe.matmul(ps[64 * half:64 * half + 64, col:col + 128],
                                        A.v[block % 2][:, at:at + 64],
                                        pt[:, j * 128:(j + 1) * 128], start=True, stop=True)
                ins.then_inc(A.weighed, 1)

            if l == 0:
                pe.wait_ge(A.w_loaded, 16 * A.n_loads)
            else:
                pe.wait_ge(wo1_in, 16)
                pe.wait_ge(aw_split, 2)
                pe.wait_ge(bank6.read, bank6.done(("head", H - 1)))
                pe.wait_ge(layers[0][1].hi_done, layers[0][1].per * E0)
            values = A.side_at[-1]
            if l == 0:
                for job in range(2):
                    qk_job(0, job)
                    side_job(*values[job])
                for job in values[2:]:
                    side_job(*job)
            score(0)
            score(1)
            for job in range(4):
                if l:
                    qk_job(1, job)
                    if job % 2 == 0:
                        side_job(*values[job // 2])
                if job % 2:
                    score(2 + job // 2)
            for job in A.qk_at(-1):
                qk_job(*job)
            if l:
                pe.wait_ge(layers[0][1].y_added, NG * (E0 - 1))
            for n in range(NU + 2):
                if n + AHEAD < NU:
                    score(n + AHEAD)
                if n < NU:
                    turn(n)
                    for job in A.qk_at(n):
                        qk_job(*job)
                    for job in A.early_sides(n):
                        side_job(*job)
                if NU <= n < NU + layers[l][1].early:
                    pe.wait_ge(A.exped, NU)
                    hidden(pe, layers[l][1], 0, 0, n - NU, 0)
                if n >= 2:
                    weigh(n - 2)
                if n < NU:
                    for job in A.late_sides(n):
                        side_job(*job)
                for item in norm_at(l, n, "turn"):
                    norm_turn(pe, *item)
                for phase, g in norm_at(l, n, "y_turn"):
                    y_turn(pe, 0, g)
                r, steps = route_at(l, n)
                if "rows_turn" in steps:
                    rows_tensor(pe, r)
                if "logits" in steps:
                    logits_tensor(pe, r)
            for job in A.side_at[NU]:
                side_job(*job)

        def att_scalar(act, A):
            l = A.l

            def exps(n):
                act.wait_ge(A.maxed, n + 1)
                until(act, A.turned, n - SLOTS + 1)
                until(act, A.inverted, n - SLOTS + 1)
                for j in range(4):
                    col = (n % SLOTS) * 4 + j
                    ins = act.activation(A.p[n % SLOTS][:, j * 128:(j + 1) * 128],
                                         bank[n % 2][:, j * 128:(j + 1) * 128], ACT.Exp,
                                         bias=negmax[:, col:col + 1], scale=1.0, accum_out=total[:, col:col + 1])
                ins.then_inc(A.exped, 1)

            def copy_out(n):
                act.wait_ge(A.turned, n + 1)
                until(act, A.weighed, n - 1)
                act.activation(A.pt[n % 2][:, :], bank[2 + n % 2][:, :], ACT.Copy).then_inc(A.turned_a, 1)

            def qk_copy(block, job):
                if l:
                    keys_high(act, A, block, job)
                    return
                g, turns, w = block // QUADS, A.qk_turns(block, job), "kq"[job]
                act.wait_ge(turns.filled, turns.upto(("qk", l, block, job)))
                out_, bias, scale = ((A.q, A.bq_scaled, SCALE0) if w == "q" else (A.all_k, A.bias["k"], 1.0))
                until(act, A.scored, UNITS * (g - 1))
                act.activation(out_[g % 2][:, :], turns.psum[:, :], ACT.Identity, bias=bias[:, :],
                               scale=scale).then_inc(turns.read, 1)

            if l == 0:
                act.wait_ge(bias_scaled, 1)
                for job in range(2):
                    qk_copy(0, job)
            exps(0)
            for job in range(4):
                if l:
                    qk_copy(1, job)
                if job == 0:
                    exps(1)
            exps(2)
            for n in range(NU + 1):
                if l:
                    for job in A.qk_at(n - 1):
                        qk_copy(*job)
                if n + 3 < NU:
                    exps(n + 3)
                if l == 0:
                    for job in A.qk_at(n - 1):
                        qk_copy(*job)
                for item in norm_at(l, n, "copy"):
                    norm_copy(act, *item)
                if n and (l or (n - 1) % 2 == 0):
                    copy_out(n - 1)

        def att_pool(p, A):
            l = A.l

            def head_keys(block, j):
                g, quad = divmod(block, QUADS)
                p.wait_ge(bank6.read, bank6.done(("qk", 0, QUADS * g, 0)))
                until(p, A.scored, BPG * (block - 1))
                kk = A.k[block % 2][:, :].rearrange("p (b h s) -> p b h s", b=BPG, h=4)[:, :, j, :]
                ins = p.tensor_tensor(kk, A.all_k[g % 2][:, :].rearrange("p (b s) -> p b s", b=BPG),
                                      masks[:, 4 * quad + j:4 * quad + j + 1].rearrange("p (b s) -> p b s", b=1)
                                      .to_broadcast([128, BPG, S]), ALU.mult)
                if j == 3:
                    ins.then_inc(A.keys_p, 1)

            if l == 0:
                for block in range(2):
                    for j in (2, 3):
                        head_keys(block, j)
            for n in range(NU):
                s = (n % SLOTS) * 4
                p.wait_ge(A.inverted, n + 1)
                pr = A.p[n % SLOTS][:, :].rearrange("p (h s) -> p h s", h=4)
                p.tensor_tensor(pr, pr, rtotal[:, s:s + 4].rearrange("p (h o) -> p h o", o=1).to_broadcast([128, 4, 128]),
                                ALU.mult).then_inc(A.normed, 1)
                if l == 0 and n % 4 < 2 and n // 4 + 2 < QUADS * NG:
                    head_keys(n // 4 + 2, 2 + n % 4)
                if n == 4:
                    if l == 0:
                        p.wait_ge(late_in, 16 * N_LATE)
                    add_bias(p, 2 * l, 0)
                for item in norm_at(l, n, "power"):
                    norm_power(p, *item)
                for item in norm_at(l, n, "bias"):
                    add_bias(p, *item)
                if 11 <= n < 11 + 8 * 4 and n % 4 == 3:
                    e, piece = divmod((n - 11) // 4, 4)
                    split_weights(p, layers[l][1], e, e, piece // 2, piece % 2)

        def att_vector(v, A):
            l = A.l

            def row_max(n):
                v.wait_ge(A.scored, n + 1)
                until(v, A.exped, n - SLOTS + 1)
                s = (n % SLOTS) * 4
                v.tensor_reduce(negmax[:, s:s + 4], bank[n % 2][:, :].rearrange("p (h s) -> p h s", h=4),
                                AX_X, ALU.max, negate=True).then_inc(A.maxed, 1)

            def invert(n):
                v.wait_ge(A.exped, n + 1)
                until(v, A.normed, n - SLOTS + 1)
                s = (n % SLOTS) * 4
                v.reciprocal(rtotal[:, s:s + 4], total[:, s:s + 4]).then_inc(A.inverted, 1)

            def copy_out(n):
                v.wait_ge(A.turned, n + 1)
                until(v, A.weighed, n - 1)
                v.tensor_copy(A.pt[n % 2][:, :], bank[2 + n % 2][:, :]).then_inc(A.turned_v, 1)

            def out_copy(chunk):
                v.wait_ge(A.weighed, A.out_per * (chunk + 1))
                g, c = divmod(chunk, UNITS // A.out_per)
                if g and c in ((1,) if l == 0 else (0, 1)):
                    batches = BPG if l == 0 or c else 2
                    v.wait_ge(bank7.filled, bank7.done(("O", l, BPG * (g - 1) + batches - 1)))
                ps = bank[4 + chunk % 2]
                if l == 0:
                    v.tensor_copy(A.ot[:, group(A.ot_slot(g, c))], ps[:, :]).then_inc(A.out_copied, 1)
                else:
                    quad, half = divmod(c, 2)
                    o = A.ot[:, 2 * quad * GROUP:(2 * quad + 2) * GROUP].rearrange("p (i s) -> p i s", i=2)
                    v.tensor_copy(o[:, :, half * 256:(half + 1) * 256],
                                  ps[:, :].rearrange("p (i s) -> p i s", i=2)).then_inc(A.out_copied, 1)

            def head_keys(block, j):
                g, quad = divmod(block, QUADS)
                v.wait_ge(bank6.read, bank6.done(("qk", 0, QUADS * g, 0)))
                until(v, A.scored, BPG * (block - 1))
                kk = A.k[block % 2][:, :].rearrange("p (b h s) -> p b h s", b=BPG, h=4)[:, :, j, :]
                ins = v.tensor_scalar(kk, A.all_k[g % 2][:, :].rearrange("p (b s) -> p b s", b=BPG),
                                      masks[:, 4 * quad + j:4 * quad + j + 1], None, ALU.mult)
                if j == 1:
                    ins.then_inc(A.keys_v, 1)

            def side(name, item):
                turns = A.side_turns(name, item)
                v.wait_ge(turns.filled, turns.upto((name, l, item)))
                side_ps = turns.psum[:, 0:D if name == "O" or l == 0 else 512]
                if name == "V" and l == 0:
                    b = item % BPG
                    until(v, A.weighed, UNITS * (item // BPG) - BPG + b + 1 if item >= BPG else 0)
                    if item < BPG:
                        v.wait_ge(A.cleared, 1)
                    vv = A.v[:, b * 512:(b + 1) * 512].rearrange("p (h c) -> p h c", h=H)[:, :, 0:HD0]
                    v.tensor_tensor(vv, side_ps.rearrange("p (h c) -> p h c", h=H),
                                    A.bv[:, :].rearrange("p (h c) -> p h c", h=H), ALU.add).then_inc(turns.read, 1)
                elif name == "V":
                    block, b = divmod(item, BPG)
                    until(v, A.weighed, item + 1 - 8 + 1)
                    v.tensor_copy(A.v[block % 2][:, b * 256:(b + 2) * 256], side_ps).then_inc(turns.read, 1)
                else:
                    t = item
                    xs = x[:, t * D:(t + 1) * D]
                    v.wait_ge(bo_added, NG * l + t // BPG + 1)
                    v.tensor_tensor(xs, side_ps, xs, ALU.add).then_inc(turns.read, 1)

            if l == 0:
                for block in range(2):
                    for j in range(2):
                        head_keys(block, j)
                for job in A.side_at[-1]:
                    side(*job)
            row_max(0)
            row_max(1)
            for i in range(4):
                if l:
                    keys_low(v, A, 1, i)
                    if i % 2 == 0:
                        side(*A.side_at[-1][i // 2])
                if i % 2:
                    row_max(2 + i // 2)
            for n in range(2):
                invert(n)
            for n in range(NU + 3):
                if 0 < n <= NU:
                    for job in A.early_sides(n - 1):
                        side(*job)
                if n + 2 < NU:
                    invert(n + 2)
                if l == 0 and n <= NU and n and (n - 1) % 2:
                    copy_out(n - 1)
                if l and n <= NU:
                    for job in A.qk_at(n - 1):
                        keys_low(v, A, *job)
                if n + AHEAD < NU:
                    row_max(n + AHEAD)
                if 0 < n <= NU:
                    for job in A.late_sides(n - 1):
                        side(*job)
                for phase, g in norm_at(l, n, "y_add"):
                    y_add(v, 0, g)
                r, steps = route_at(l, n)
                if "rows_copy" in steps:
                    rows_vector(v, r)
                if 0 in steps:
                    route_vector(v, r, 0)
                if l == 0 and n % 4 in (1, 3) and n // 4 + 2 < QUADS * NG:
                    head_keys(n // 4 + 2, n % 4 // 2)
                if l == 0 and n in CONTEXT_STEPS:
                    split_context(v, CONTEXT_STEPS.index(n))
                if n > 2 and (n - 2) % A.out_per == 0:
                    out_copy((n - 2) // A.out_per - 1)
                for item in norm_at(l, n, "split"):
                    norm_split(v, *item)
                for item in norm_at(l, n, "stats"):
                    norm_stats(v, *item)
                for item in norm_at(l, n, "scale"):
                    norm_scale(v, *item)
                for step in steps:
                    if isinstance(step, int) and step:
                        route_vector(v, r, step)
            for job in A.side_at[NU]:
                side(*job)

        class Experts:
            def __init__(self, l, stack):
                self.l = l
                n = f"_x{l}"
                s = lambda name: sem(name + n)
                self.n = E0 if l == 0 else E
                self.nb = JOBS0 if l == 0 else JOBS1
                self.per = self.nb * NG
                self.early = 2 - l
                hid = HID0 if l == 0 else HID1
                self.width = lambda hb: min(128, hid - 128 * hb)
                names = ("in", "out") if l == 0 else ("in", "up", "out")
                self.at = {w: k * hid for k, w in enumerate(names)}
                self.cols = (len(names) - 1) * hid + self.nb * 128
                b_ = lambda name, shape, dt=F32: sb(name + n, shape, dt, stack)
                self.gate = [b_(f"gate{i}_", [128, TOK]) for i in range(2)]
                self.act = [b_(f"act{i}_", [128, GROUP]) for i in range(RING)] if l else None
                self.h = [b_(f"h{i}_", [128, GROUP]) for i in range(RING)]
                self.h_hi = [b_(f"hh{i}_", [128, GROUP], F32R) for i in range(RING)]
                self.h_lo = [b_(f"hl{i}_", [128, GROUP], F32R) for i in range(RING)]
                if l == 0:
                    self.aw_raw = {w: b_("aw_raw_" + w, [128, INNER1]) for w in "vqk"}
                self.bias_in = [s("bias_in_a"), s("bias_in_b")]
                self.route = 0 if l == 0 else NG
                self.logits_at, self.rows_at = (5, 15) if l == 0 else (6, 10)
                self.steps_at = ({6: (0,), 7: (1,), 8: (2,), 9: (3,), 11: (4, 5), 12: (6, 7)} if l == 0 else
                                 {7: (0, 1, 2), 8: (3, 4, 5), 9: (6, 7)})
                last = self.per if l else 0
                self.turn_at = [last + self.nb * (g + 1) + LAG + (3, 1)[l] for g in range(1 if l == 0 else 2)]
                self.weighted = b_("weighted", [128, GROUP])
                self.w_in, self.rounded, self.raw_split = s("w_in"), s("rounded"), s("raw_split")
                self.gate_in = [s("gate_in_a"), s("gate_in_b")]
                self.gate_part_in = [s(f"gate_part{g}_in") for g in range(NG)]
                self.h_ps, self.acted, self.multiplied = s("h_ps"), s("acted"), s("multiplied")
                self.hi_done, self.lo_done, self.h_used = s("hi_done"), s("lo_done"), s("h_used")
                self.y_added, self.y_read = s("y_added"), s("y_read")

            def heads_at(self, first, j):
                return {14 + 2 * i: i for i in range(H // 2)}.get(j) if first and self.l == 0 else None

            def keys_at(self, last, j):
                return {2: 0, 4: 1, 6: 2, 9: 3}.get(j) if last and self.l == 0 else None

            def w(self, halves, i, name, cols, rows=128):
                return halves[i][0:rows, self.at[name] + cols.start:self.at[name] + cols.stop]

            def loop(self, eng, body):
                body(0, 2)
                with eng.Fori(1, (self.n - 1) // 2) as p:
                    body(p, 2)
                body((self.n - 1) // 2, 2 - self.n % 2)

        def load_weights(sp, X, e):
            until(sp, X.raw_split, 2 * e)
            sp.dma_start(w_raw[:, 0:X.cols], a[f"w_{X.l}"][span(e * 128, 128), :]).then_inc(X.w_in, 16)

        def load_gates(sp, X, s, i):
            until(sp, X.y_read, NG * (s - 1))
            e = s - 1 if X.l == 0 else s
            row = gate_rows[X.l, span(e, 1), :] if not isinstance(e, int) else gate_rows[X.l, e:e + 1, :]
            sp.dma_start(X.gate[i][:, :], row.to_broadcast([128, TOK])).then_inc(X.gate_in[i], 16)

        def load_gates_part(sp, X, g):
            sp.dma_start(X.gate[1 - X.l][:, group(g)], gate_rows[X.l, 0:1, group(g)].to_broadcast([128, GROUP])
                         ).then_inc(X.gate_part_in[g], 16)

        def ffn_sync(sp, X):
            def body(pair, n):
                for i in range(n):
                    s = 2 * pair + i
                    load_weights(sp, X, s)
                    if X.l == 0:
                        sp.wait_ge(X.hi_done, X.per * (s - 1))
                        sp.dma_start(b1[i][:, :], a["b1"][span(s * 128, 128), :]).then_inc(X.bias_in[i], 16)
                    load_gates(sp, X, s, i)
            if X.l == 0:
                for w in "kqv":
                    sp.dma_start(X.aw_raw[w][:, :], a[f"w{w}1"]).then_inc(aw_in, 16)
                sp.dma_start(wo1[:, :], a["wo1"]).then_inc(wo1_in, 16)
                route_sync(sp, 0)
                for g in range(NG):
                    load_gates_part(sp, X, g)
            else:
                for g in range(NG - 1):
                    load_gates_part(sp, X, g)
                route_sync(sp, NG)
                load_gates_part(sp, X, NG - 1)
                load_gates(sp, X, 1, 1)
            with sp.Fori(1, (X.n - 1) // 2) as p:
                body(p, 2)
            body((X.n - 1) // 2, 2 - X.n % 2)

        def split_weights(p, X, e, i, chunk, low):
            c = slice(chunk * X.cols // 2, (chunk + 1) * X.cols // 2)
            if not low:
                if chunk == 0:
                    p.wait_ge(X.w_in, 16 * (e + 1))
                until(p, X.h_used, X.per * (e - 1))
                p.tensor_tensor(w_hi[i][:, c], w_raw[:, c], zeros[:, 0:X.cols // 2], ALU.add).then_inc(X.rounded, 1)
                return
            p.wait_ge(X.rounded, 2 * e + chunk + 1)
            p.tensor_tensor(w_lo[i][:, c], w_raw[:, c], w_hi[i][:, c].bitcast(F32), ALU.subtract).then_inc(X.raw_split, 1)

        def ffn_pool(p, X):
            norm_power(p, 2 * X.l + 1, NG - 1)
            if X.l == 0:
                route_power(p)

            def body(pair, n):
                for i in range(n):
                    for chunk in range(2):
                        for low in range(2):
                            split_weights(p, X, 2 * pair + i, i, chunk, low)
            with p.Fori(1, (X.n - 1) // 2) as pair:
                body(pair, 2)
            body((X.n - 1) // 2, 2 - X.n % 2)
            if X.l == 0:
                p.wait_ge(aw_in, 48)
                for i in range(2):
                    c = slice(512 * i, 512 * (i + 1))
                    p.tensor_tensor(wv_hi[:, c], X.aw_raw["v"][:, c], zeros[:, 0:512], ALU.add).then_inc(pool_own, 1)
                    p.wait_ge(pool_own, i + 2)
                    p.tensor_tensor(wv_lo[:, c], X.aw_raw["v"][:, c], wv_hi[:, c].bitcast(F32),
                                    ALU.subtract).then_inc(aw_split, 1)
                norm_power(p, 2, 0)

        def head_weights_tensor(pe, X, i):
            pe.wait_ge(aw_in, 48)
            for k, turns in enumerate((bank7, bank6)):
                rows = slice(HD1 * k, HD1 * (k + 1))
                until(pe, turns.read, turns.before(("head", 2 * i + k)))
                pe.matmul(turns.psum[:, 0:D], X.aw_raw["k"][rows, tile(i)], X.aw_raw["q"][rows, tile(i)],
                          start=True, stop=True).then_inc(turns.filled, 1)

        def head_weights_vector(v, i):
            for k, turns in enumerate((bank7, bank6)):
                c = tile(2 * i + k)
                v.wait_ge(turns.filled, turns.upto(("head", 2 * i + k)))
                done = seq(v.tensor_scalar(wkq_hi[:, c], turns.psum[:, 0:D], SCALE1, None, ALU.mult))
                v.wait_ge(dve, done)
                v.scalar_tensor_tensor(out=wkq_lo[:, c], in0=turns.psum[:, 0:D], scalar=SCALE1,
                                       in1=wkq_hi[:, c].bitcast(F32), op0=ALU.mult, op1=ALU.subtract
                                       ).then_inc(turns.read, 1)

        def hidden(pe, X, e, i, j, base):
            tg, hb = divmod(j % X.per, X.nb)
            width = X.width(hb)
            m = slice(tg * GROUP, (tg + 1) * GROUP)
            c = slice(hb * 128, hb * 128 + width)
            if j % X.per == 0:
                pe.wait_ge(X.raw_split, 2 * e + 2)
            if isinstance(e, int) and e == 0 and j == 2 - X.l:
                for spare in (bank2, bank3):
                    pe.wait_ge(spare.read, len(spare.order))
            if isinstance(e, int) and e == 0 and hb == 0:
                pe.wait_ge(xt_ready, SPLIT_NO[2 * X.l + 1, tg] + 1)
            if X.l == 0:
                until(pe, X.hi_done, base + j - 3)
                three(pe, bank[j % 4][0:width, :], X.w(w_hi, i, "in", c), X.w(w_lo, i, "in", c),
                      xt_hi[:, m], xt_lo[:, m]).then_inc(X.h_ps, 1)
            else:
                until(pe, X.multiplied, base + j - 1)
                for k, w in enumerate(("in", "up")):
                    ins = three(pe, bank[2 * (j % 2) + k][0:width, :], X.w(w_hi, i, w, c), X.w(w_lo, i, w, c),
                                xt_hi[:, m], xt_lo[:, m])
                ins.then_inc(X.h_ps, 1)

        def ffn_tensor(pe, X):
            def outward(j, base, ubase):
                i = (j // X.per) % 2
                tg, hb = divmod(j % X.per, X.nb)
                width = X.width(hb)
                unit = j // X.nb
                ps = bank[4 + unit % 2]
                if hb == 0:
                    until(pe, X.y_read, ubase + unit - 1)
                pe.wait_ge(X.hi_done, base + j + 1)
                pe.wait_ge(X.lo_done, base + j + 1)
                wc = slice(hb * 128, (hb + 1) * 128)
                hi, lo = X.w(w_hi, i, "out", wc, width), X.w(w_lo, i, "out", wc, width)
                hh, hl = X.h_hi[j % RING][0:width, :], X.h_lo[j % RING][0:width, :]
                pe.matmul(ps[:, :], lo, hh, start=(hb == 0), stop=False)
                pe.matmul(ps[:, :], hi, hl, start=False, stop=False)
                pe.matmul(ps[:, :], hi, hh, start=False, stop=(hb == X.nb - 1)).then_inc(X.h_used, 1)

            def body(pair, n):
                e0 = 2 * pair
                base, ubase = X.per * e0, NG * e0
                first, last = isinstance(pair, int) and pair == 0, isinstance(pair, int) and pair > 0
                for j in range(n * X.per):
                    if not (first and j < X.early):
                        hidden(pe, X, e0 + j // X.per, j // X.per, j, base)
                    if not (first and j < LAG):
                        outward(j - LAG, base, ubase)
                    if first and j == 3:
                        norm_turn(pe, 2 * X.l + 1, NG - 1)
                    if first and j == X.logits_at:
                        logits_tensor(pe, X.route)
                    if first and j == X.rows_at:
                        rows_tensor(pe, X.route)
                    if X.heads_at(first, j) is not None:
                        head_weights_tensor(pe, X, X.heads_at(first, j))
                    if X.keys_at(last, j) is not None:
                        keys_tensor(pe, layers[1][0], 0, X.keys_at(last, j))
                    if last and j in X.turn_at:
                        y_turn(pe, X.l, X.turn_at.index(j))
                    if last and X.l == 0 and j == X.turn_at[0] + 5:
                        norm_turn(pe, 2, 0)
            X.loop(pe, body)
            tail = X.n - 1 if X.n % 2 else X.n - 2
            for j in range(X.per * X.n - LAG, X.per * X.n):
                outward(j - X.per * tail, X.per * tail, NG * tail)
            if X.l:
                for g in range(len(X.turn_at), NG):
                    y_turn(pe, 1, g)

        def ffn_scalar(act, X):
            def body(pair, n):
                e0 = 2 * pair
                base = X.per * e0
                first, last = isinstance(pair, int) and pair == 0, isinstance(pair, int) and pair > 0
                for j in range(n * X.per):
                    if first and j == 4:
                        norm_copy(act, 2 * X.l + 1, NG - 1)
                    if X.keys_at(last, j - 1) is not None:
                        keys_high(act, layers[1][0], 0, X.keys_at(last, j - 1))
                    e, hb = e0 + j // X.per, j % X.nb
                    width = X.width(hb)
                    r = j % RING
                    act.wait_ge(X.h_ps, base + j + 1)
                    if X.l == 0:
                        bias = b1[j // X.per][:, hb:hb + 1]
                        if j % X.per == 0:
                            act.wait_ge(X.bias_in[j // X.per], pair * 16 + 16)
                        until(act, X.lo_done, base + j - 3)
                        act.activation(X.h[r][:, :], bank[r][:, :], ACT.Gelu, bias=bias).then_inc(X.acted, 1)
                        until(act, X.h_used, base + j - 3)
                        act.activation(X.h_hi[r][:, :], bank[r][:, :], ACT.Gelu, bias=bias).then_inc(X.hi_done, 1)
                        continue
                    until(act, X.multiplied, base + j - 3)
                    act.activation(X.act[r][0:width, :], bank[2 * (j % 2)][0:width, :], ACT.Silu).then_inc(X.acted, 1)
                    if not (isinstance(e0, int) and e0 == 0 and j == 0):
                        high(base, j - 1)
            def high(base, j):
                width, r = X.width(j % X.nb), j % RING
                act.wait_ge(X.multiplied, base + j + 1)
                until(act, X.h_used, base + j - 3)
                act.activation(X.h_hi[r][0:width, :], X.h[r][0:width, :], ACT.Copy).then_inc(X.hi_done, 1)
            X.loop(act, body)
            if X.l == 0:
                norm_copy(act, 2, 0)
            else:
                high(0, X.per * X.n - 1)

        def ffn_vector(v, X):
            norm_stats(v, 2 * X.l + 1, NG - 1)

            def low(base, j):
                width, r = X.width(j % X.nb), j % RING
                v.wait_ge(X.hi_done, base + j + 1)
                until(v, X.h_used, base + j - 3)
                v.tensor_tensor(X.h_lo[r][0:width, :], X.h[r][0:width, :], X.h_hi[r][0:width, :].bitcast(F32),
                                ALU.subtract).then_inc(X.lo_done, 1)

            def gather(p, j):
                e0, base, ubase = 2 * p, 2 * X.per * p, 2 * NG * p
                unit = j // X.nb
                tg = unit % NG
                i = (unit // NG) % 2
                e = e0 + unit // NG
                m = slice(tg * GROUP, (tg + 1) * GROUP)
                v.wait_ge(X.h_used, base + j + 1)
                ps = bank[4 + unit % 2]
                if isinstance(e, int) and e == 0:
                    if X.l == 0:
                        v.tensor_scalar(y[:, m], ps[:, :], b2[:, 0:1], None, ALU.add).then_inc(X.y_read, 1)
                    else:
                        v.wait_ge(X.gate_part_in[tg], 16)
                        v.tensor_tensor(y[:, m], ps[:, :], X.gate[0][:, m], ALU.mult).then_inc(X.y_read, 1)
                    return
                if X.l == 0 and isinstance(e, int) and e == 1:
                    v.wait_ge(X.gate_part_in[tg], 16)
                elif tg == 0:
                    v.wait_ge(X.gate_in[i], 16 * (p + i * X.l))
                gate = X.gate[i][:, m]
                until(v, X.y_added, ubase + unit - NG)
                if X.l == 0:
                    v.scalar_tensor_tensor(out=X.weighted[:, :], in0=ps[:, :], scalar=b2[:, span(e, 1)], in1=gate,
                                           op0=ALU.add, op1=ALU.mult).then_inc(X.y_read, 1)
                else:
                    v.tensor_tensor(X.weighted[:, :], ps[:, :], gate, ALU.mult).then_inc(X.y_read, 1)
                v.wait_ge(X.y_read, ubase + unit + 1)
                v.tensor_tensor(y[:, m], y[:, m], X.weighted[:, :], ALU.add).then_inc(X.y_added, 1)

            def body(p, n):
                base = 2 * X.per * p
                zero, last = isinstance(p, int) and p == 0, isinstance(p, int) and p > 0
                for j in range(n * X.per):
                    if zero and j == 2:
                        norm_scale(v, 2 * X.l + 1, NG - 1)
                    if zero and j == 5:
                        norm_split(v, 2 * X.l + 1, NG - 1)
                    if zero:
                        for step in X.steps_at.get(j, ()):
                            route_vector(v, X.route, step)
                    if zero and j == X.rows_at + 1:
                        rows_vector(v, X.route)
                    if X.heads_at(zero, j - 1) is not None:
                        head_weights_vector(v, X.heads_at(zero, j - 1))
                    if X.keys_at(last, j - 1) is not None:
                        keys_low(v, layers[1][0], 0, X.keys_at(last, j - 1))
                    if last and j - 1 in X.turn_at:
                        y_add(v, X.l, X.turn_at.index(j - 1))
                    if last and X.l == 0 and j == X.turn_at[0] + 1:
                        norm_stats(v, 2, 0)
                    if last and X.l == 0 and j == X.turn_at[0] + 3:
                        norm_scale(v, 2, 0)
                    if X.l == 0:
                        low(base, j)
                    else:
                        width, r = X.width(j % X.nb), j % RING
                        v.wait_ge(X.acted, base + j + 1)
                        until(v, X.hi_done, base + j - 3)
                        v.tensor_tensor(X.h[r][0:width, :], bank[2 * (j % 2) + 1][0:width, :], X.act[r][0:width, :],
                                        ALU.mult).then_inc(X.multiplied, 1)
                        if not (zero and j == 0):
                            low(base, j - 1)
                    done = j - LAG - 1
                    if (done + 1) % X.nb == 0 and not (zero and done < 0):
                        gather(p, done)
            X.loop(v, body)
            tail = X.n - 1 if X.n % 2 else X.n - 2
            rest = X.per * (X.n - tail)
            if X.l:
                low(X.per * tail, rest - 1)
            else:
                norm_split(v, 2, 0)
            for done in range(rest - LAG - 1, rest):
                if (done + 1) % X.nb == 0:
                    gather(tail // 2, done)
            if X.l:
                for g in range(len(X.turn_at), NG):
                    y_add(v, 1, g)

        layers = []
        for l in range(2):
            with ExitStack() as st:
                A = Attention(l, st)
            with ExitStack() as st:
                X = Experts(l, st)
            layers.append((A, X))

        A0 = layers[0][0]
        A0.loads = [(A0.w["k"][:, :], a["wk0"]), (A0.w["q"][:, :], a["wq0"]), (A0.bias["k"][:, :], a["bk"]),
                    (A0.bias["q"][:, :], a["bq"]), (A0.w["v"][:, :], a["wv0"]),
                    (A0.bv[:, :], a["bv"].to_broadcast([128, D])), (A0.wo[:, :], a["wo0"])]
        A0.n_loads = len(A0.loads)
        constants = [(masks, "masks"), (ident, "ident")]
        late = [(expert_no, "expert_no"), (gw[0], "gw0"), (gw[1], "gw1"), (b2, "b2")]
        N_LATE = len(late) + 3

        block = ctx.enter_context(nc.Block())

        @block.tensor
        def _(pe):
            pe.wait_ge(const_in, 16 * len(constants))
            norm_turn(pe, 0, 0)
            for l, (A, X) in enumerate(layers):
                att_tensor(pe, A)
                if l == 0:
                    pe.wait_ge(late_in, 16 * N_LATE)
                ffn_tensor(pe, X)

        @block.sync
        def _(sp):
            def load_x(g):
                t = slice(g * BPG, (g + 1) * BPG)
                sp.dma_start(x[:, group(g)].rearrange("s (b d) -> s b d", b=BPG), a["x"][t].rearrange("b s d -> s b d")
                             ).then_inc(x_in[g], 16)

            def load_ct(g):
                sp.dma_start(ct[:, group(g)], a["ct"][:, group(g)]).then_inc(ct_in[g], 16)

            load_x(0)
            load_ct(0)
            for dst, src in A0.loads[:2]:
                sp.dma_start(dst, src).then_inc(A0.w_loaded, 16)
            for dst, name in constants:
                sp.dma_start(dst[:, :], a[name]).then_inc(const_in, 16)
            for dst, src in A0.loads[2:]:
                sp.dma_start(dst, src).then_inc(A0.w_loaded, 16)
            for dst, name in late:
                sp.dma_start(dst[:, :], a[name]).then_inc(late_in, 16)
            sp.dma_start(gb[:, :], a["gb"].to_broadcast([128, E])).then_inc(late_in, 16)
            for l in range(2):
                sp.dma_start(bo[l][:, :], a[f"bo{l}"].to_broadcast([128, D])).then_inc(late_in, 16)
            for g in range(1, NG):
                load_x(g)
                load_ct(g)
            for l, (A, X) in enumerate(layers):
                if l:
                    sp.wait_ge(layers[0][1].raw_split, 2 * E0)
                load_weights(sp, X, 0)
                load_weights(sp, X, 1)
                if l == 0:
                    for i in range(2):
                        sp.dma_start(b1[i][:, :], a["b1"][i * 128:(i + 1) * 128]).then_inc(X.bias_in[i], 16)
                else:
                    for r in range(1, NG):
                        route_sync(sp, r)
                sp.wait_ge(X.h_ps, X.early + 1)
                ffn_sync(sp, X)
            for g in range(NG):
                sp.wait_ge(bank7.read, bank7.done(("y", 1, g)))
                t = slice(g * BPG, (g + 1) * BPG)
                sp.dma_start(out[t].rearrange("b s d -> s b d"), x[:, group(g)].rearrange("s (b d) -> s b d", b=BPG)
                             ).then_inc(finished, 16)
            sp.wait_ge(finished, 16 * NG)

        @block.scalar
        def _(act):
            norm_copy(act, 0, 0)
            for A, X in layers:
                att_scalar(act, A)
                ffn_scalar(act, X)

        @block.gpsimd
        def _(p):
            p.memset(minus_half[:, :], -0.5).then_inc(pool_own, 1)
            p.memset(euler[:, :], float(np.e))
            p.memset(zeros[:, :], 0.0)
            p.memset(A0.v[:, :], 0.0).then_inc(A0.cleared, 1)
            p.wait_ge(pool_own, 1)
            norm_power(p, 0, 0)
            p.wait_ge(A0.cleared, 1)
            p.wait_ge(const_in, 16 * len(constants))
            for A, X in layers:
                att_pool(p, A)
                ffn_pool(p, X)

        @block.vector
        def _(v):
            norm_stats(v, 0, 0)
            norm_scale(v, 0, 0)
            v.wait_ge(A0.w_loaded, 16 * A0.n_loads)
            v.tensor_scalar(A0.bq_scaled[:, :], A0.bias["q"][:, :], SCALE0, None, ALU.mult).then_inc(bias_scaled, 1)
            v.wait_ge(const_in, 16 * len(constants))
            for l, (A, X) in enumerate(layers):
                att_vector(v, A)
                if l == 0:
                    v.wait_ge(late_in, 16 * N_LATE)
                ffn_vector(v, X)


def kernel(**inputs):
    import concourse.bacc as bacc
    from concourse.bass_utils import run_bass_kernel_spmd

    f = {n: np.asarray(v) for n, v in inputs.items()}
    rows = np.arange(128)
    masks = np.stack([rows // HD0 == h for h in range(H)], axis=1)

    def chunks(w, width):
        e, hid, o = w.shape
        whole = np.zeros((e, width, o), w.dtype)
        whole[:, :hid] = w
        return whole.reshape(e, width // 128, 128, o).transpose(0, 2, 1, 3).reshape(e * 128, -1)

    wo0 = np.zeros((QUADS, 4, 32, D), f["L0_xattn_Wo"].dtype)
    wo0[:, :, :HD0] = f["L0_xattn_Wo"].T.reshape(QUADS, 4, HD0, D)
    arrays = {
        "x": f["x"],
        "ct": f["ctx_1024"].reshape(TOK, D).T,
        "masks": masks.astype(np.float32),
        "ident": np.eye(128, dtype=np.float32),
        "expert_no": np.broadcast_to(np.repeat(np.arange(E, dtype=np.float32), B), (128, E * B)),
        "wq0": f["L0_xattn_Wq"].T, "wk0": f["L0_xattn_Wk"].T,
        "wv0": f["L0_xattn_Wv"].T,
        "wo0": wo0.reshape(QUADS, 128, D).transpose(1, 0, 2).reshape(128, QUADS * D),
        "bq": f["L0_xattn_bq"].reshape(D, 1), "bk": f["L0_xattn_bk"].reshape(D, 1),
        "bv": f["L0_xattn_bv"].reshape(1, D),
        "bo0": f["L0_xattn_bo"].reshape(1, D), "bo1": f["L1_xattn_bo"].reshape(1, D),
        "gw0": f["L0_ffn_gate_w"], "gb": f["L0_ffn_gate_b"].reshape(1, E),
        "w_0": np.concatenate([np.concatenate([f["L0_ffn_ws1"][None], f["L0_ffn_w1"]]).reshape(E0 * 128, HID0),
                               chunks(np.concatenate([f["L0_ffn_ws2"][None], f["L0_ffn_w2"]]), HID0)], axis=1),
        "b1": np.concatenate([f["L0_ffn_bs1"][None], f["L0_ffn_b1"]]).reshape(E0, JOBS0, 128).transpose(0, 2, 1)
                .reshape(E0 * 128, JOBS0),
        "b2": np.concatenate([f["L0_ffn_bs2"][None], f["L0_ffn_b2"]]).T,
        "wq1": f["L1_xattn_Wq"].T.reshape(H // 2, 128, D).transpose(1, 0, 2).reshape(128, -1),
        "wk1": f["L1_xattn_Wk"].T.reshape(H // 2, 128, D).transpose(1, 0, 2).reshape(128, -1),
        "wv1": f["L1_xattn_Wv"],
        "wo1": f["L1_xattn_Wo"].reshape(8, 128, D).transpose(1, 0, 2).reshape(128, 8 * D),
        "gw1": f["L1_ffn_Wg"].T,
        "w_1": np.concatenate([f["L1_ffn_W1"].transpose(0, 2, 1).reshape(E * 128, HID1),
                               f["L1_ffn_W2"].transpose(0, 2, 1).reshape(E * 128, HID1),
                               chunks(f["L1_ffn_W3"].transpose(0, 2, 1), JOBS1 * 128)], axis=1),
    }
    nc = bacc.Bacc("TRN2", target_bir_lowering=False, num_devices=1)
    named, aps = {}, {}
    for name, value in arrays.items():
        value = np.ascontiguousarray(value)
        named["in_" + name] = value
        aps[name] = nc.dram_tensor("in_" + name, value.shape, mybir.dt.from_np(value.dtype), kind="ExternalInput").ap()
    result = nc.dram_tensor("result", (B, S, D), F32, kind="ExternalOutput").ap()
    build(nc, aps, result)
    r = run_bass_kernel_spmd(nc, [named], core_ids=[0])
    return r.results[0]["result"]
```
